# Optimizing a Trainium2 kernel written in Bass

```python
import numpy as np
import jax
import jax.numpy as jnp

def _softmax(x, axis=-1):
    return jax.nn.softmax(x, axis=axis)

def _gelu(x):
    return jax.nn.gelu(x, approximate=True)

def _silu(x):
    return jax.nn.silu(x)

def _sigmoid(x):
    return jax.nn.sigmoid(x)

def _layernorm(x, axis=-1, eps=1e-05):
    m = jnp.mean(x, axis=axis, keepdims=True)
    v = jnp.var(x, axis=axis, keepdims=True)
    return (x - m) / jnp.sqrt(v + eps)

def _scatter_add(tgt, idx, src, axis=0):
    return tgt.at[idx].add(src)

def _segment_sum(src, seg, n):
    return jax.ops.segment_sum(src, seg, n)
kernel_name = 'mk_conv_seq_d2_conv_nchw192_r2_f984e7'

def setup_inputs(seed: int=0):
    np.random.seed(seed)
    _w = jnp.asarray

    def _rec_inputs():
        import jax
        import jax.numpy as jnp
        _gk = jax.random.key(seed)
        x = -0.0001476 + 0.9999 * jax.random.normal(jax.random.fold_in(_gk, 1), (32, 96, 56, 56), jnp.float32)
        return x
    x = _rec_inputs()

    def _L0_conv_setup():
        import jax, jax.numpy as jnp
        import numpy as np
        C = 96
        DCT = 7
        EPS = 1e-05
        LOW_X = [0, 0, 1, 1, 0, 2, 2, 1, 2, 0, 3, 4, 0, 1, 3, 0, 1, 2, 3, 4, 5, 0, 1, 2, 3, 4, 5, 6, 1, 2, 3, 4]
        LOW_Y = [0, 1, 0, 1, 2, 0, 1, 2, 2, 3, 0, 0, 4, 3, 1, 5, 4, 3, 2, 1, 0, 6, 5, 4, 3, 2, 1, 0, 6, 5, 4, 3]

        def _dct_basis():
            t = jnp.arange(DCT, dtype=jnp.float32)
            fx = jnp.array(LOW_X, dtype=jnp.float32)
            fy = jnp.array(LOW_Y, dtype=jnp.float32)

            def bf(freq):
                r = jnp.cos(jnp.pi * freq[:, None] * (t[None, :] + 0.5) / DCT) / jnp.sqrt(jnp.float32(DCT))
                return jnp.where(freq[:, None] == 0, r, r * jnp.sqrt(jnp.float32(2.0)))
            bx, by = (bf(fx), bf(fy))
            return bx[:, :, None] * by[:, None, :]
        key = jax.random.key(seed)
        ks = jax.random.split(key, 16)
        n, h, w = (32, 56, 56)
        return {'x': jax.random.normal(ks[0], (n, C, h, w), jnp.float32), 'wg1': jax.random.normal(ks[1], (32, C), jnp.float32) * (2.0 / C) ** 0.5, 'bn2_g': jax.random.uniform(ks[2], (32,), jnp.float32, 0.8, 1.2), 'bn2_b': jax.random.normal(ks[3], (32,), jnp.float32) * 0.1, 'bn2_m': jax.random.normal(ks[4], (32,), jnp.float32) * 0.1, 'bn2_v': jax.random.uniform(ks[5], (32,), jnp.float32, 0.5, 1.5), 'wg2': jax.random.normal(ks[6], (32, 32), jnp.float32) * (2.0 / 32) ** 0.5, 'bg2': jax.random.normal(ks[7], (32,), jnp.float32) * 0.1, 'beta': jax.random.uniform(ks[8], (1,), jnp.float32, 0.05, 0.25), 'w1d': jax.random.normal(ks[9], (C, C, 3), jnp.float32) * (2.0 / (3 * C)) ** 0.5, 'b1d': jax.random.normal(ks[10], (C,), jnp.float32) * 0.1, 'bn1_g': jax.random.uniform(ks[11], (C,), jnp.float32, 0.8, 1.2), 'bn1_b': jax.random.normal(ks[12], (C,), jnp.float32) * 0.1, 'bn1_m': jax.random.normal(ks[13], (C,), jnp.float32) * 0.1, 'bn1_v': jax.random.uniform(ks[14], (C,), jnp.float32, 0.5, 1.5)}
    _L0_conv_all = _L0_conv_setup()
    _L0_conv_in = {k: v for k, v in _L0_conv_all.items() if k in ('wg1', 'bn2_g', 'bn2_b', 'bn2_m', 'bn2_v', 'wg2', 'bg2', 'beta', 'w1d', 'b1d', 'bn1_g', 'bn1_b', 'bn1_m', 'bn1_v')}
    del _L0_conv_all

    def _L1_conv_setup():
        import jax, jax.numpy as jnp
        import numpy as np
        DIM = 96
        K = 3
        RED = 4
        B, H, W = (4, 128, 128)
        EPS = 1e-05

        def _make_mask():
            m = np.ones((DIM, 1, K, K), np.float32)
            m[:, :, K // 2, K // 2:] = 0.0
            m[:, :, K // 2 + 1:] = 0.0
            return jnp.asarray(m)
        MASK = _make_mask()
        key = jax.random.key(seed)
        ks = jax.random.split(key, 4)
        r = DIM // RED
        return {'x': jax.random.normal(ks[0], (B, DIM, H, W), jnp.float32), 'w1': jax.random.normal(ks[1], (r, DIM), jnp.float32) * 0.05, 'gamma': jnp.ones((r,), jnp.float32), 'beta': jnp.zeros((r,), jnp.float32), 'running_mean': jnp.zeros((r,), jnp.float32), 'running_var': jnp.ones((r,), jnp.float32), 'w2': jax.random.normal(ks[2], (DIM * K * K, r), jnp.float32) * 0.05, 'b2': jnp.zeros((DIM * K * K,), jnp.float32), 'bias': jnp.zeros((DIM,), jnp.float32)}
    _L1_conv_all = _L1_conv_setup()
    _L1_conv_in = {k: v for k, v in _L1_conv_all.items() if k in ('w1', 'gamma', 'beta', 'running_mean', 'running_var', 'w2', 'b2', 'bias')}
    del _L1_conv_all
    return {'x': x, 'L0_conv_wg1': _L0_conv_in['wg1'], 'L0_conv_bn2_g': _L0_conv_in['bn2_g'], 'L0_conv_bn2_b': _L0_conv_in['bn2_b'], 'L0_conv_bn2_m': _L0_conv_in['bn2_m'], 'L0_conv_bn2_v': _L0_conv_in['bn2_v'], 'L0_conv_wg2': _L0_conv_in['wg2'], 'L0_conv_bg2': _L0_conv_in['bg2'], 'L0_conv_beta': _L0_conv_in['beta'], 'L0_conv_w1d': _L0_conv_in['w1d'], 'L0_conv_b1d': _L0_conv_in['b1d'], 'L0_conv_bn1_g': _L0_conv_in['bn1_g'], 'L0_conv_bn1_b': _L0_conv_in['bn1_b'], 'L0_conv_bn1_m': _L0_conv_in['bn1_m'], 'L0_conv_bn1_v': _L0_conv_in['bn1_v'], 'L1_conv_w1': _L1_conv_in['w1'], 'L1_conv_gamma': _L1_conv_in['gamma'], 'L1_conv_beta': _L1_conv_in['beta'], 'L1_conv_running_mean': _L1_conv_in['running_mean'], 'L1_conv_running_var': _L1_conv_in['running_var'], 'L1_conv_w2': _L1_conv_in['w2'], 'L1_conv_b2': _L1_conv_in['b2'], 'L1_conv_bias': _L1_conv_in['bias']}

def reference(x, L0_conv_wg1, L0_conv_bn2_g, L0_conv_bn2_b, L0_conv_bn2_m, L0_conv_bn2_v, L0_conv_wg2, L0_conv_bg2, L0_conv_beta, L0_conv_w1d, L0_conv_b1d, L0_conv_bn1_g, L0_conv_bn1_b, L0_conv_bn1_m, L0_conv_bn1_v, L1_conv_w1, L1_conv_gamma, L1_conv_beta, L1_conv_running_mean, L1_conv_running_var, L1_conv_w2, L1_conv_b2, L1_conv_bias):
    import jax
    import jax.numpy as jnp

    def _L0_conv_ref(x, wg1, bn2_g, bn2_b, bn2_m, bn2_v, wg2, bg2, beta, w1d, b1d, bn1_g, bn1_b, bn1_m, bn1_v):
        import jax, jax.numpy as jnp
        import numpy as np
        C = 96
        DCT = 7
        EPS = 1e-05
        LOW_X = [0, 0, 1, 1, 0, 2, 2, 1, 2, 0, 3, 4, 0, 1, 3, 0, 1, 2, 3, 4, 5, 0, 1, 2, 3, 4, 5, 6, 1, 2, 3, 4]
        LOW_Y = [0, 1, 0, 1, 2, 0, 1, 2, 2, 3, 0, 0, 4, 3, 1, 5, 4, 3, 2, 1, 0, 6, 5, 4, 3, 2, 1, 0, 6, 5, 4, 3]

        def _dct_basis():
            t = jnp.arange(DCT, dtype=jnp.float32)
            fx = jnp.array(LOW_X, dtype=jnp.float32)
            fy = jnp.array(LOW_Y, dtype=jnp.float32)

            def bf(freq):
                r = jnp.cos(jnp.pi * freq[:, None] * (t[None, :] + 0.5) / DCT) / jnp.sqrt(jnp.float32(DCT))
                return jnp.where(freq[:, None] == 0, r, r * jnp.sqrt(jnp.float32(2.0)))
            bx, by = (bf(fx), bf(fy))
            return bx[:, :, None] * by[:, None, :]
        n, c, h, w = x.shape
        g = jnp.einsum('nchw,oc->nohw', x, wg1)
        g = (g - bn2_m[None, :, None, None]) * (bn2_g / jnp.sqrt(bn2_v + EPS))[None, :, None, None] + bn2_b[None, :, None, None]
        g = jax.nn.relu(g).mean(axis=(2, 3))
        xg = g @ wg2.T + bg2
        xg = jax.nn.relu(jnp.tanh(xg)) + beta
        xg0 = jax.lax.stop_gradient(xg[0])
        s = xg0.sum()
        p_mid = jnp.round(xg0[:31] / s * c)
        param = jnp.concatenate([jnp.zeros(1, jnp.float32), p_mid, (jnp.float32(c) - p_mid.sum())[None]])
        ch = jnp.arange(c, dtype=jnp.float32)
        basis = _dct_basis()
        filt = jnp.zeros((c, DCT, DCT), jnp.float32)
        for i in range(32):
            m = (ch >= param[i]) & (ch < param[i + 1])
            filt = jnp.where(m[:, None, None], basis[i], filt)
        xp = x.reshape(n, c, DCT, h // DCT, DCT, w // DCT).mean(axis=(3, 5))
        y = jnp.sum(xp * filt[None], axis=(2, 3))
        y = y @ w1d[:, :, 1].T + b1d
        y = (y - bn1_m) * (bn1_g / jnp.sqrt(bn1_v + EPS)) + bn1_b
        y = jax.nn.relu(y)
        return x * y[:, :, None, None] + x

    def _L1_conv_ref(x, w1, gamma, beta, running_mean, running_var, w2, b2, bias):
        import jax, jax.numpy as jnp
        import numpy as np
        DIM = 96
        K = 3
        RED = 4
        B, H, W = (4, 128, 128)
        EPS = 1e-05

        def _make_mask():
            m = np.ones((DIM, 1, K, K), np.float32)
            m[:, :, K // 2, K // 2:] = 0.0
            m[:, :, K // 2 + 1:] = 0.0
            return jnp.asarray(m)
        MASK = _make_mask()
        b, c, h, w = x.shape
        pooled = x.mean(axis=(2, 3))
        t = pooled @ w1.T
        t = gamma * (t - running_mean) * jax.lax.rsqrt(running_var + EPS) + beta
        t = jax.nn.relu(t)
        wt = t @ w2.T + b2
        wt = wt.reshape(b * DIM, 1, K, K) * jnp.tile(MASK, (b, 1, 1, 1))
        out = jax.lax.conv_general_dilated(x.reshape(1, b * c, h, w), wt, window_strides=(1, 1), padding=((1, 1), (1, 1)), feature_group_count=b * DIM, dimension_numbers=('NCHW', 'OIHW', 'NCHW'))
        out = out + jnp.tile(bias, (b,))[None, :, None, None]
        return out.reshape(b, c, h, w)

    def _gn(v, G=32, eps=1e-05):
        B_, C_, H_, W_ = v.shape
        g = v.reshape(B_, G, C_ // G, H_, W_)
        m = jnp.mean(g, axis=(2, 3, 4), keepdims=True)
        s = jnp.var(g, axis=(2, 3, 4), keepdims=True)
        return ((g - m) / jnp.sqrt(s + eps)).reshape(v.shape)

    def _ln_c(v, eps=1e-06):
        m = jnp.mean(v, axis=1, keepdims=True)
        s = jnp.var(v, axis=1, keepdims=True)
        return (v - m) / jnp.sqrt(s + eps)

    def _ln_t(v, eps=1e-05):
        m = jnp.mean(v, axis=-1, keepdims=True)
        s = jnp.var(v, axis=-1, keepdims=True)
        return (v - m) / jnp.sqrt(s + eps)

    def _to_tokens(v):
        B_, C_, H_, W_ = v.shape
        return v.reshape(B_, C_, H_ * W_).transpose(0, 2, 1)

    def _from_tokens(t, like):
        B_, C_, H_, W_ = like.shape
        return t.transpose(0, 2, 1).reshape(B_, C_, H_, W_)
    x = _L0_conv_ref(x, L0_conv_wg1, L0_conv_bn2_g, L0_conv_bn2_b, L0_conv_bn2_m, L0_conv_bn2_v, L0_conv_wg2, L0_conv_bg2, L0_conv_beta, L0_conv_w1d, L0_conv_b1d, L0_conv_bn1_g, L0_conv_bn1_b, L0_conv_bn1_m, L0_conv_bn1_v)
    x = _L1_conv_ref(x, L1_conv_w1, L1_conv_gamma, L1_conv_beta, L1_conv_running_mean, L1_conv_running_var, L1_conv_w2, L1_conv_b2, L1_conv_bias)
    return x

_drawn_inputs = setup_inputs


def setup_inputs(seed=0):
    import zlib

    import numpy as np

    out = dict(_drawn_inputs(seed))
    spreads = {'L1_conv_gamma': (1.0, 0.2),
     'L1_conv_beta': (0.0, 0.1),
     'L1_conv_running_mean': (0.0, 0.1),
     'L1_conv_running_var': (1.0, 0.6),
     'L1_conv_b2': (0.0, 0.1),
     'L1_conv_bias': (0.0, 0.1)}
    factors = {'L0_conv_wg1': 5.063,
     'L0_conv_bn2_g': 6.095,
     'L0_conv_bn2_v': 4.202,
     'L0_conv_wg2': 3.75,
     'L0_conv_bg2': 5.367,
     'L0_conv_w1d': 3.513,
     'L0_conv_bn1_g': 4.579,
     'L0_conv_bn1_v': 4.308,
     'L1_conv_w1': 3.489}
    for name, (base, spread) in spreads.items():
        noise = np.random.default_rng([zlib.crc32(name.encode()), seed]).standard_normal(out[name].shape)
        drawn = base * np.exp(spread * noise) if base else spread * noise
        out[name] = jnp.asarray(drawn.astype(out[name].dtype))
    for name, factor in factors.items():
        out[name] = (out[name] * factor).astype(out[name].dtype)
    return out
```

```python
from contextlib import ExitStack

import concourse.bass as bass
from concourse import mybir

NIMG, C, H, W = 32, 96, 56, 56
HW = H * W
P = 128
QUAD = 32
PER = C // QUAD
GROUP = P // QUAD
NGROUP = NIMG // GROUP
SLOTS = 2
TURNS = NGROUP // SLOTS
TILES = SLOTS * PER
DCT = 7
BLK = H // DCT
CELLS = DCT * DCT
NF = 32
RED = 24
TAPS = 4
WHOLE_TAP = 1
EPS = 1e-05
ROUND = 12582912.0

PE_CHUNK = 7
PE_CHUNKS = 3
PE_ROWS = PE_CHUNK * PE_CHUNKS
V_ROWS = H - PE_ROWS
CHUNK = PE_CHUNK * W
BANK = 512
GATE_CHUNK = 392
GATE_HALF = 4
PAD = W

K_IDENT = 0
K_ONES = K_IDENT + P
K_SHIFT = K_ONES + NF
K_TRI = K_SHIFT + 2 * NF
K_EDGE = K_TRI + NF
K_CHAN = K_EDGE + 2
K_BASIS = K_CHAN + PER * P
K_END = K_BASIS + CELLS


def tap_windows(row0, rows, tap):
    if tap == 3:
        return slice(row0 + 1, row0 + 1 + rows), slice(0, W - 1), slice(1, W)
    if tap == 0:
        return slice(row0, row0 + rows), slice(0, W - 1), slice(1, W)
    if tap == 2:
        return slice(row0, row0 + rows), slice(1, W), slice(0, W - 1)
    return slice(row0, row0 + rows), slice(0, W), slice(0, W)


def build(nc, x, consts, rowp, gatep, hidp, wg1t, wg2t, w1dt, w1t, w2t, b2t, out):
    fp32 = mybir.dt.float32
    ALU = mybir.AluOpType
    ACT = mybir.ActivationFunctionType
    AX = mybir.AxisListType

    x_tiles = x.rearrange("n c h w -> (n c) (h w)").rearrange("(g p t) f -> g t p f", p=P, t=PER)
    out_tiles = out.rearrange("n c h w -> (n c) (h w)").rearrange("(g p t) f -> g t p f", p=P, t=PER)
    x_image0 = x[0, :, :, :].rearrange("c h w -> c (h w)")

    with ExitStack() as ctx:
        def sb(name, shape):
            return ctx.enter_context(nc.sbuf_tensor(name, shape, fp32))

        def sem(name):
            return ctx.enter_context(nc.semaphore(name))

        xin = sb("xin", [P, SLOTS, PER, PAD + HW])
        xout = sb("xout", [P, SLOTS, PER, HW])
        k = sb("k", [P, K_END])
        row_par = sb("row_par", [P, 6, PER])
        gate_par = sb("gate_par", [NF, 6])
        hid_par = sb("hid_par", [C, 4])
        w_gate1 = sb("w_gate1", [C, NF])
        w_gate2 = sb("w_gate2", [NF, NF])
        w_mix = sb("w_mix", [P, PER, PER, P])
        w_hid = sb("w_hid", [P, PER, C])
        w_tap = sb("w_tap", [C + 1, PER * TAPS, P])
        filt = sb("filt", [P, PER, CELLS])
        pooled = sb("pooled", [P, PER, 2, CELLS])
        sums = sb("sums", [P, PER, 2])
        mixed = sb("mixed", [P, PER])
        gain = sb("gain", [P, PER])
        total = sb("total", [P, PER])
        hidden = sb("hidden", [C + 1, 1])
        coef = sb("coef", [P, SLOTS, PER, TAPS])
        diag = sb("diag", [P, PER, TAPS, P])
        expo = sb("expo", [P, PER])
        rs_row = sb("rs_row", [P, PER])
        rs_gate = sb("rs_gate", [NF, 1])
        rs_hid = sb("rs_hid", [C, 1])
        a_row = sb("a_row", [P, PER])
        b_row = sb("b_row", [P, PER])
        a_gate = sb("a_gate", [NF, 1])
        b_gate = sb("b_gate", [NF, 1])
        a_hid = sb("a_hid", [C, 1])
        b_hid = sb("b_hid", [C, 1])
        gate_sum = sb("gate_sum", [NF, 2])
        gate_act = sb("gate_act", [NF, 1])
        xg = sb("xg", [NF, 1])
        inv_s = sb("inv_s", [NF, 1])
        share = sb("share", [NF, 1])
        count = sb("count", [NF, 1])
        bounds = sb("bounds", [NF, 2])
        above = sb("above", [NF, PER * P])
        hit = sb("hit", [NF, PER * P])
        chosen = sb("chosen", [NF, PER, P])

        ident = k[:, K_IDENT:K_IDENT + P]
        ones = k[0:NF, K_ONES:K_ONES + NF]
        shift = k[0:NF, K_SHIFT:K_SHIFT + 2 * NF].rearrange("p (a b) -> p a b", a=2)
        tri = k[0:NF, K_TRI:K_TRI + NF]
        edge = k[0:NF, K_EDGE:K_EDGE + 2]
        chan = k[0:NF, K_CHAN:K_CHAN + PER * P]
        basis = k[0:NF, K_BASIS:K_BASIS + CELLS]
        image0 = xout[0:C, SLOTS - 1, PER - 1, :]

        banks = ctx.enter_context(nc.psum_tensor("banks", [P, 8, BANK], fp32))
        p_mixed = banks[:, 6, 0:PER]
        p_hidden = banks[0:C, 6, 8:9]
        p_taps = banks[:, 6, 16:16 + PER * TAPS]
        p_gate2 = banks[0:NF, 7, 0:1]
        p_s = banks[0:NF, 7, 1:2]
        p_bounds = banks[0:NF, 7, 2:4]
        p_later = banks[0:NF, 7, 8:8 + PER * P]
        p_filt = banks[:, 6, 0:PER * CELLS]

        def grid(slot, t):
            return xin[:, slot, t, :].rearrange("p (r c) -> p r c", c=W)

        def result(slot, t):
            return xout[:, slot, t, :].rearrange("p (r c) -> p r c", c=W)

        consts_in = sem("consts_in")
        image0_in = sem("image0_in")
        weights_in = sem("weights_in")
        loaded = [[sem(f"loaded_{s}_{t}") for t in range(PER)] for s in range(SLOTS)]
        stored = [[sem(f"stored_{s}_{t}") for t in range(PER)] for s in range(SLOTS)]
        zeroed = sem("zeroed")
        expo_set = sem("expo_set")
        rsqrt_done = sem("rsqrt_done")
        fold = sem("fold")
        folded = sem("folded")
        gate_mm = sem("gate_mm")
        gate_relu = sem("gate_relu")
        gate2_mm = sem("gate2_mm")
        gate_tanh = sem("gate_tanh")
        xg_done = sem("xg_done")
        s_mm = sem("s_mm")
        assign = sem("assign")
        counted = sem("counted")
        bounds_mm = sem("bounds_mm")
        hit_done = sem("hit_done")
        later_mm = sem("later_mm")
        chosen_done = sem("chosen_done")
        filt_mm = sem("filt_mm")
        filt_done = sem("filt_done")
        cells_done = sem("cells_done")
        chain = sem("chain")
        sums_done = sem("sums_done")
        mixed_mm = sem("mixed_mm")
        total_done = sem("total_done")
        hidden_mm = sem("hidden_mm")
        hidden_done = sem("hidden_done")
        taps_mm = sem("taps_mm")
        coef_done = sem("coef_done")
        diag_done = sem("diag_done")
        first_tap = sem("first_tap")
        tap_done = sem("tap_done")
        rows_done = sem("rows_done")
        conv_mm = sem("conv_mm")
        conv_out = sem("conv_out")

        block = ctx.enter_context(nc.Block())

        @block.sync
        def _(sp):
            sp.dma_start(image0, x_image0).then_inc(image0_in, 16)
            sp.dma_start(w_gate1[:, :], wg1t).then_inc(consts_in, 16)
            sp.dma_start(gate_par[:, :], gatep).then_inc(consts_in, 16)
            sp.dma_start(w_gate2[:, :], wg2t).then_inc(consts_in, 16)
            sp.dma_start(row_par[:, :, :], rowp).then_inc(consts_in, 16)
            sp.dma_start(hid_par[:, :], hidp).then_inc(consts_in, 16)
            sp.dma_start(k[:, :], consts).then_inc(consts_in, 16)
            for t in range(PER):
                sp.dma_start(xin[:, 0, t, PAD:], x_tiles[0, t]).then_inc(loaded[0][t], 16)
            sp.wait_ge(zeroed, 2)
            for n in range(GROUP):
                q = slice(QUAD * n, QUAD * (n + 1))
                r = slice(RED * n, RED * (n + 1))
                sp.dma_start(w_mix[q, :, :, q], w1dt).then_inc(weights_in, 16)
                sp.dma_start(w_hid[q, :, r], w1t).then_inc(weights_in, 16)
                sp.dma_start(w_tap[r, :, q], w2t).then_inc(weights_in, 16)
                sp.dma_start(w_tap[C:C + 1, :, q], b2t).then_inc(weights_in, 16)
            for t in range(PER):
                sp.dma_start(xin[:, 1, t, PAD:], x_tiles[1, t]).then_inc(loaded[1][t], 16)

            def exchange(turn, last):
                for s in range(SLOTS):
                    for t in range(PER):
                        sp.wait_ge(rows_done, TILES * turn + PER * s + t + 1)
                        sp.wait_ge(conv_out, TILES * turn + PER * s + t + 1)
                        if not last:
                            sp.dma_start(xin[:, s, t, PAD:], x_tiles[SLOTS * turn + SLOTS + s, t]).then_inc(loaded[s][t], 16)
                        sp.dma_start(out_tiles[SLOTS * turn + s, t], xout[:, s, t, :]).then_inc(stored[s][t], 16)

            with sp.Fori(0, TURNS - 1) as turn:
                exchange(turn, False)
            exchange(TURNS - 1, True)
            for s in range(SLOTS):
                for t in range(PER):
                    sp.wait_ge(stored[s][t], 16 * TURNS)

        @block.gpsimd
        def _(pool):
            nc.gpsimd.memset(expo[:, :], -0.5).then_inc(expo_set, 1)
            nc.gpsimd.memset(w_mix[:, :, :, :], 0.0)
            nc.gpsimd.memset(w_hid[:, :, :], 0.0).then_inc(zeroed, 1)
            nc.gpsimd.memset(w_tap[:, :, :], 0.0).then_inc(zeroed, 1)
            nc.gpsimd.memset(xin[:, :, :, 0:PAD], 0.0).then_inc(zeroed, 1)
            pool.wait_ge(zeroed, 3)
            nc.gpsimd.memset(hidden[C:C + 1, :], 1.0).then_inc(zeroed, 1)
            pool.wait_ge(zeroed, 4)
            pool.wait_ge(expo_set, 1)
            pool.wait_ge(fold, 3)
            nc.gpsimd.tensor_tensor(rs_gate[:, :], b_gate[:, :], expo[0:NF, 0:1], ALU.pow).then_inc(rsqrt_done, 1)
            nc.gpsimd.tensor_tensor(rs_row[:, :], b_row[:, :], expo[:, :], ALU.pow).then_inc(rsqrt_done, 1)
            nc.gpsimd.tensor_tensor(rs_hid[:, :], b_hid[:, :], expo[0:C, 0:1], ALU.pow).then_inc(rsqrt_done, 1)

        @block.vector
        def _(dve):
            vec = nc.vector
            dve.wait_ge(consts_in, 96)
            vec.tensor_scalar(b_gate[:, :], gate_par[:, 3:4], EPS, None, ALU.add).then_inc(fold, 1)
            vec.tensor_scalar(b_row[:, :], row_par[:, 4, :], EPS, None, ALU.add).then_inc(fold, 1)
            vec.tensor_scalar(b_hid[:, :], hid_par[:, 3:4], EPS, None, ALU.add).then_inc(fold, 1)
            dve.wait_ge(rsqrt_done, 3)
            vec.tensor_tensor(a_gate[:, :], gate_par[:, 0:1], rs_gate[:, :], ALU.mult).then_inc(fold, 1)
            vec.tensor_tensor(a_row[:, :], row_par[:, 2, :], rs_row[:, :], ALU.mult).then_inc(fold, 1)
            vec.tensor_tensor(b_row[:, :], row_par[:, 0, :], row_par[:, 1, :], ALU.subtract).then_inc(fold, 1)
            vec.tensor_tensor(a_hid[:, :], hid_par[:, 0:1], rs_hid[:, :], ALU.mult).then_inc(fold, 1)
            dve.wait_ge(fold, 7)
            vec.tensor_tensor(b_gate[:, :], gate_par[:, 2:3], a_gate[:, :], ALU.mult).then_inc(fold, 1)
            vec.tensor_tensor(b_row[:, :], b_row[:, :], a_row[:, :], ALU.mult).then_inc(fold, 1)
            vec.tensor_tensor(b_hid[:, :], hid_par[:, 2:3], a_hid[:, :], ALU.mult).then_inc(fold, 1)
            dve.wait_ge(fold, 10)
            vec.tensor_tensor(b_gate[:, :], gate_par[:, 1:2], b_gate[:, :], ALU.subtract).then_inc(folded, 1)
            vec.tensor_tensor(b_row[:, :], b_row[:, :], row_par[:, 3, :], ALU.add).then_inc(folded, 1)
            vec.tensor_tensor(b_hid[:, :], hid_par[:, 1:2], b_hid[:, :], ALU.subtract).then_inc(folded, 1)
            vec.tensor_scalar(a_hid[:, :], a_hid[:, :], 1.0 / HW, None, ALU.mult).then_inc(folded, 1)

            def pool_tile(group_loads, slot, t):
                dve.wait_ge(loaded[slot][t], 16 * group_loads)
                vec.tensor_reduce(pooled[:, t, 1, :].rearrange("p (a b) -> p a b", a=DCT),
                                  xin[:, slot, t, PAD:].rearrange("p (a b c d) -> p a c b d", a=DCT, b=BLK, c=DCT),
                                  AX.XY, ALU.add).then_inc(cells_done, 1)

            def sum_cells(g):
                dve.wait_ge(cells_done, PER * (g + 1))
                vec.tensor_tensor(pooled[:, :, 0, :], pooled[:, :, 1, :], filt[:, :, :], ALU.mult).then_inc(chain, 1)
                dve.wait_ge(chain, 4 * g + 1)
                vec.tensor_reduce(sums[:, :, :], pooled[:, :, :, :], AX.X, ALU.add).then_inc(sums_done, 1)

            def gain_steps(g):
                dve.wait_ge(mixed_mm, g + 1)
                vec.tensor_tensor(mixed[:, :], p_mixed, a_row[:, :], ALU.mult).then_inc(chain, 1)
                dve.wait_ge(chain, 4 * g + 2)
                vec.tensor_tensor(mixed[:, :], mixed[:, :], b_row[:, :], ALU.add).then_inc(chain, 1)
                dve.wait_ge(chain, 4 * g + 3)
                vec.tensor_scalar(gain[:, :], mixed[:, :], 0.0, 1.0, ALU.max, ALU.add).then_inc(chain, 1)
                dve.wait_ge(chain, 4 * g + 4)
                vec.tensor_tensor(total[:, :], gain[:, :], sums[:, :, 1], ALU.mult).then_inc(total_done, 1)

            def coef_step(g, slot):
                dve.wait_ge(taps_mm, g + 1)
                vec.tensor_tensor(coef[:, slot, :, :], p_taps.rearrange("p (t k) -> p t k", t=PER),
                                  gain[:, :].rearrange("p (t k) -> p t k", k=1).broadcast_to([P, PER, TAPS]), ALU.mult).then_inc(coef_done, 1)

            def tap(slot, t, which):
                rows, cols, ocols = tap_windows(0, V_ROWS, which)
                acc = result(slot, t)[:, 0:V_ROWS, ocols]
                return vec.scalar_tensor_tensor(out=acc, in0=grid(slot, t)[:, rows, cols],
                                                scalar=coef[:, slot, t, which:which + 1],
                                                in1=acc, op0=ALU.mult, op1=ALU.add)

            dve.wait_ge(gate_tanh, 1)
            vec.tensor_scalar(xg[:, :], gate_act[:, :], 0.0, gate_par[:, 5:6], ALU.max, ALU.add).then_inc(xg_done, 1)
            dve.wait_ge(s_mm, 1)
            vec.reciprocal(inv_s[:, :], p_s).then_inc(assign, 1)
            dve.wait_ge(assign, 1)
            vec.tensor_scalar(share[:, :], xg[:, :], inv_s[:, 0:1], float(C), ALU.mult, ALU.mult).then_inc(assign, 1)
            dve.wait_ge(assign, 2)
            vec.tensor_scalar(count[:, :], share[:, :], ROUND, -ROUND, ALU.add, ALU.add).then_inc(counted, 1)
            dve.wait_ge(bounds_mm, 1)
            vec.tensor_tensor(bounds[:, :], p_bounds, edge, ALU.add).then_inc(assign, 1)
            dve.wait_ge(assign, 3)
            vec.tensor_scalar(above[:, :], chan, bounds[:, 0:1], None, ALU.is_ge).then_inc(assign, 1)
            dve.wait_ge(assign, 4)
            vec.scalar_tensor_tensor(out=hit[:, :], in0=chan, scalar=bounds[:, 1:2], in1=above[:, :],
                                     op0=ALU.is_lt, op1=ALU.mult).then_inc(hit_done, 1)
            dve.wait_ge(later_mm, 1)
            vec.scalar_tensor_tensor(out=chosen[:, :, :].rearrange("p t r -> p (t r)"), in0=p_later, scalar=0.5,
                                     in1=hit[:, :], op0=ALU.is_lt, op1=ALU.mult).then_inc(chosen_done, 1)
            for t in range(PER):
                pool_tile(1, 0, t)
            dve.wait_ge(filt_done, 1)
            sum_cells(0)
            dve.wait_ge(folded, 4)
            gain_steps(0)
            coef_step(0, 0)

            def conv(turn, s, t, between):
                tile = TILES * turn + PER * s + t
                dve.wait_ge(first_tap, tile + 1)
                tap(s, t, 0).then_inc(tap_done, 1)
                dve.wait_ge(tap_done, 2 * tile + 1)
                tap(s, t, 2).then_inc(tap_done, 1)
                between()
                dve.wait_ge(tap_done, 2 * tile + 2)
                tap(s, t, 3).then_inc(rows_done, 1)

            def turn_of(turn, last):
                for s in range(SLOTS):
                    g = SLOTS * turn + s
                    ahead = not (last and s == SLOTS - 1)
                    other = (s + 1) % SLOTS
                    loads = turn + 1 + (s + 1) // SLOTS
                    nothing = lambda: None
                    if ahead:
                        pool_tile(loads, other, 0)
                    conv(turn, s, 0, nothing)
                    if ahead:
                        pool_tile(loads, other, 1)
                        pool_tile(loads, other, 2)
                        sum_cells(g + 1)
                    conv(turn, s, 1, nothing)
                    if ahead:
                        gain_steps(g + 1)
                    conv(turn, s, 2, (lambda: coef_step(g + 1, other)) if ahead else nothing)

            with dve.Fori(0, TURNS - 1) as turn:
                turn_of(turn, False)
            turn_of(TURNS - 1, True)

        @block.scalar
        def _(act):
            sca = nc.scalar
            for half in range(2):
                if half == 0:
                    act.wait_ge(folded, 1)
                act.wait_ge(gate_mm, half + 1)
                sca.activation(banks[0:NF, GATE_HALF * half:GATE_HALF * (half + 1), 0:GATE_CHUNK],
                               banks[0:NF, GATE_HALF * half:GATE_HALF * (half + 1), 0:GATE_CHUNK], ACT.Relu,
                               bias=b_gate[:, :], scale=a_gate[:, :],
                               accum_out=gate_sum[:, half:half + 1]).then_inc(gate_relu, 1)
            act.wait_ge(gate2_mm, 1)
            sca.activation(gate_act[:, :], p_gate2, ACT.Tanh, bias=gate_par[:, 4:5],
                           scale=1.0 / HW).then_inc(gate_tanh, 1)
            act.wait_ge(filt_mm, 1)
            sca.activation(filt[:, :, :].rearrange("p t c -> p (t c)"), p_filt, ACT.Copy).then_inc(filt_done, 1)

            def hidden_relu(g):
                act.wait_ge(hidden_mm, g + 1)
                sca.activation(hidden[0:C, :], p_hidden, ACT.Relu, bias=b_hid[:, :],
                               scale=a_hid[:, :]).then_inc(hidden_done, 1)

            def start_tile(turn, s, t):
                tile = TILES * turn + PER * s + t
                act.wait_ge(coef_done, SLOTS * turn + s + 1)
                for w in range(TAPS):
                    ins = sca.activation(diag[:, t, w, :], ident, ACT.Copy, scale=coef[:, s, t, w:w + 1])
                ins.then_inc(diag_done, 1)
                if not (isinstance(turn, int) and turn == 0):
                    act.wait_ge(stored[s][t], 16 * turn)
                rows, cols, _ = tap_windows(0, V_ROWS, WHOLE_TAP)
                sca.activation(xout[:, s, t, 0:V_ROWS * W], xin[:, s, t, 0:V_ROWS * W], ACT.Identity,
                               bias=row_par[:, 5, t:t + 1], scale=coef[:, s, t, WHOLE_TAP:WHOLE_TAP + 1]).then_inc(first_tap, 1)

            def take_psum(turn, s, t):
                act.wait_ge(conv_mm, TILES * turn + PER * s + t + 1)
                first = PE_CHUNKS * ((PER * s + t) % 2)
                sca.activation(xout[:, s, t, V_ROWS * W:].rearrange("p (b f) -> p b f", f=CHUNK),
                               banks[:, first:first + PE_CHUNKS, 0:CHUNK], ACT.Identity,
                               bias=row_par[:, 5, t:t + 1]).then_inc(conv_out, 1)

            act.wait_ge(folded, 4)
            hidden_relu(0)
            start_tile(0, 0, 0)

            def turn_of(turn, last):
                for s in range(SLOTS):
                    ahead = not (last and s == SLOTS - 1)
                    start_tile(turn, s, 1)
                    take_psum(turn, s, 0)
                    start_tile(turn, s, 2)
                    take_psum(turn, s, 1)
                    if ahead:
                        hidden_relu(SLOTS * turn + s + 1)
                        start_tile(turn + (s + 1) // SLOTS, (s + 1) % SLOTS, 0)
                    take_psum(turn, s, 2)

            turn_of(0, False)
            with act.Fori(1, TURNS - 1) as turn:
                turn_of(turn, False)
            turn_of(TURNS - 1, True)

        @block.tensor
        def _(pe):
            mm = nc.tensor.matmul
            pe.wait_ge(consts_in, 96)
            pe.wait_ge(image0_in, 16)
            for half in range(2):
                for b in range(GATE_HALF * half, GATE_HALF * (half + 1)):
                    ins = mm(banks[0:NF, b, 0:GATE_CHUNK], w_gate1[:, :],
                             image0[:, GATE_CHUNK * b:GATE_CHUNK * (b + 1)], start=True, stop=True)
                ins.then_inc(gate_mm, 1)
            pe.wait_ge(gate_relu, 2)
            for half in range(2):
                ins = mm(p_gate2, w_gate2[:, :], gate_sum[:, half:half + 1], start=(half == 0), stop=(half == 1))
            ins.then_inc(gate2_mm, 1)
            pe.wait_ge(xg_done, 1)
            mm(p_s, ones, xg[:, :], start=True, stop=True).then_inc(s_mm, 1)
            pe.wait_ge(counted, 1)
            for b in range(2):
                ins = mm(p_bounds[:, b:b + 1], shift[:, b, :], count[:, :], start=True, stop=True)
            ins.then_inc(bounds_mm, 1)
            pe.wait_ge(hit_done, 1)
            mm(p_later, tri, hit[:, :], start=True, stop=True).then_inc(later_mm, 1)
            pe.wait_ge(chosen_done, 1)
            for t in range(PER):
                ins = mm(p_filt[:, CELLS * t:CELLS * (t + 1)], chosen[:, t, :], basis, start=True, stop=True)
            ins.then_inc(filt_mm, 1)
            pe.wait_ge(weights_in, 16 * 4 * GROUP)
            pe.wait_ge(zeroed, 4)

            def mix(g):
                pe.wait_ge(sums_done, g + 1)
                for to in range(PER):
                    for t in range(PER):
                        ins = mm(p_mixed[:, to:to + 1], w_mix[:, t, to, :], sums[:, t, 0:1],
                                 start=(t == 0), stop=(t == PER - 1))
                ins.then_inc(mixed_mm, 1)

            def hide(g):
                pe.wait_ge(total_done, g + 1)
                for t in range(PER):
                    ins = mm(p_hidden, w_hid[:, t, :], total[:, t:t + 1], start=(t == 0), stop=(t == PER - 1))
                ins.then_inc(hidden_mm, 1)

            def make_taps(g):
                pe.wait_ge(hidden_done, g + 1)
                for c in range(PER * TAPS):
                    ins = mm(p_taps[:, c:c + 1], w_tap[:, c, :], hidden[:, :], start=True, stop=True)
                ins.then_inc(taps_mm, 1)

            def conv_tap(s, t, chunk, which):
                bank = PE_CHUNKS * ((PER * s + t) % 2) + chunk
                rows, cols, ocols = tap_windows(V_ROWS + PE_CHUNK * chunk, PE_CHUNK, which)
                acc = banks[:, bank, 0:CHUNK].rearrange("p (r c) -> p r c", c=W)
                return mm(acc[:, :, ocols], diag[:, t, which, :], grid(s, t)[:, rows, cols],
                          start=(which == WHOLE_TAP), stop=(which == 3))

            TAP_ORDER = [WHOLE_TAP, 0, 2, 3]

            def conv_start(turn, s, t):
                pe.wait_ge(diag_done, TILES * turn + PER * s + t + 1)
                tile = TILES * turn + PER * s + t
                if isinstance(tile, int) and tile < 2:
                    return
                pe.wait_ge(conv_out, tile - 1)

            def conv(turn, s, t):
                conv_start(turn, s, t)
                for chunk in range(PE_CHUNKS):
                    for which in TAP_ORDER:
                        ins = conv_tap(s, t, chunk, which)
                ins.then_inc(conv_mm, 1)

            def conv_last(turn, s, t, g):
                mix(g)
                conv_start(turn, s, t)
                for which in TAP_ORDER:
                    conv_tap(s, t, 0, which)
                hide(g)
                conv_tap(s, t, 1, TAP_ORDER[0])
                make_taps(g)
                for which in TAP_ORDER[1:]:
                    conv_tap(s, t, 1, which)
                for which in TAP_ORDER:
                    ins = conv_tap(s, t, 2, which)
                ins.then_inc(conv_mm, 1)

            mix(0)
            hide(0)
            make_taps(0)

            def turn_of(turn, last):
                for s in range(SLOTS):
                    conv(turn, s, 0)
                    conv(turn, s, 1)
                    if last and s == SLOTS - 1:
                        conv(turn, s, 2)
                    else:
                        conv_last(turn, s, 2, SLOTS * turn + s + 1)

            turn_of(0, False)
            with pe.Fori(1, TURNS - 1) as turn:
                turn_of(turn, False)
            turn_of(TURNS - 1, True)


def constants():
    import numpy as np
    low_x = [0, 0, 1, 1, 0, 2, 2, 1, 2, 0, 3, 4, 0, 1, 3, 0, 1, 2, 3, 4, 5, 0, 1, 2, 3, 4, 5, 6, 1, 2, 3, 4]
    low_y = [0, 1, 0, 1, 2, 0, 1, 2, 2, 3, 0, 0, 4, 3, 1, 5, 4, 3, 2, 1, 0, 6, 5, 4, 3, 2, 1, 0, 6, 5, 4, 3]

    def wave(freq):
        f = np.array(freq, np.float64)[:, None]
        r = np.cos(np.pi * f * (np.arange(DCT)[None, :] + 0.5) / DCT) / np.sqrt(DCT)
        return np.where(f == 0, r, r * np.sqrt(2.0))

    k = np.zeros((P, K_END), np.float32)
    k[:, K_IDENT:K_IDENT + P] = np.eye(P)
    k[:NF, K_ONES:K_ONES + NF] = 1.0
    low, high = np.zeros((NF, NF)), np.zeros((NF, NF))
    for i in range(NF - 1):
        low[i, i + 1] = 1.0
        high[i, i] = 1.0
        high[i, NF - 1] = -1.0
    k[:NF, K_SHIFT:K_SHIFT + NF] = low
    k[:NF, K_SHIFT + NF:K_SHIFT + 2 * NF] = high
    k[NF - 1, K_EDGE + 1] = C
    k[:NF, K_TRI:K_TRI + NF] = np.tril(np.ones((NF, NF)), -1)
    rows = np.arange(P)
    for t in range(PER):
        k[:NF, K_CHAN + P * t:K_CHAN + P * (t + 1)] = PER * (rows % QUAD) + t
    basis = wave(low_x)[:, :, None] * wave(low_y)[:, None, :]
    k[:NF, K_BASIS:K_BASIS + CELLS] = basis.reshape(NF, CELLS) / (BLK * BLK)
    return k


def kernel(x, L0_conv_wg1, L0_conv_bn2_g, L0_conv_bn2_b, L0_conv_bn2_m, L0_conv_bn2_v, L0_conv_wg2,
           L0_conv_bg2, L0_conv_beta, L0_conv_w1d, L0_conv_b1d, L0_conv_bn1_g, L0_conv_bn1_b, L0_conv_bn1_m,
           L0_conv_bn1_v, L1_conv_w1, L1_conv_gamma, L1_conv_beta, L1_conv_running_mean,
           L1_conv_running_var, L1_conv_w2, L1_conv_b2, L1_conv_bias):
    import numpy as np
    import concourse.bacc as bacc
    from concourse.bass_utils import run_bass_kernel_spmd as run

    a = np.asarray
    per_row = np.stack([a(v).reshape(QUAD, PER) for v in (L0_conv_b1d, L0_conv_bn1_m, L0_conv_bn1_g,
                                                          L0_conv_bn1_b, L0_conv_bn1_v, L1_conv_bias)], axis=1)
    tap_weights = a(L1_conv_w2).reshape(QUAD, PER, 9, RED)[:, :, :TAPS, :]
    tap_bias = a(L1_conv_b2).reshape(QUAD, PER, 9)[:, :, :TAPS]
    arrays = {
        "x": a(x),
        "consts": constants(),
        "rowp": np.tile(per_row, (GROUP, 1, 1)),
        "gatep": np.stack([a(L0_conv_bn2_g), a(L0_conv_bn2_b), a(L0_conv_bn2_m), a(L0_conv_bn2_v),
                           a(L0_conv_bg2), np.repeat(a(L0_conv_beta), NF)], axis=1),
        "hidp": np.tile(np.stack([a(L1_conv_gamma), a(L1_conv_beta), a(L1_conv_running_mean),
                                  a(L1_conv_running_var)], axis=1), (GROUP, 1)),
        "wg1t": a(L0_conv_wg1).T,
        "wg2t": a(L0_conv_wg2).T,
        "w1dt": a(L0_conv_w1d)[:, :, 1].reshape(QUAD, PER, QUAD, PER).transpose(2, 3, 1, 0),
        "w1t": a(L1_conv_w1).T.reshape(QUAD, PER, RED),
        "w2t": tap_weights.transpose(3, 1, 2, 0).reshape(RED, PER * TAPS, QUAD),
        "b2t": tap_bias.transpose(1, 2, 0).reshape(1, PER * TAPS, QUAD),
    }
    arrays = {name: np.ascontiguousarray(v) for name, v in arrays.items()}
    nc = bacc.Bacc("TRN2", target_bir_lowering=False, num_devices=1)
    args = [nc.dram_tensor(name, v.shape, mybir.dt.float32, kind="ExternalInput").ap() for name, v in arrays.items()]
    out = nc.dram_tensor("out", (NIMG, C, H, W), mybir.dt.float32, kind="ExternalOutput").ap()
    build(nc, *args, out)
    r = run(nc, [arrays], core_ids=[0])
    return r.results[0]["out"]
```

```python
from contextlib import ExitStack

import concourse.bass as bass
from concourse import mybir

NIMG, C, H, W = 32, 96, 56, 56
HW = H * W
P = 128
QUAD = 32
PER = C // QUAD
GROUP = P // QUAD
NGROUP = NIMG // GROUP
SLOTS = 2
TURNS = NGROUP // SLOTS
TILES = SLOTS * PER
DCT = 7
BLK = H // DCT
CELLS = DCT * DCT
NF = 32
RED = 24
HID = 32
TAPS = 4
WHOLE_TAP = 1
EPS = 1e-05
ROUND = 12582912.0

CHUNKS = 3
CHUNK_ROWS = [7, 8, 7]
HEAD_ROWS = [6, 8, 7]
LAST_ROWS = [6, 6, 6]
HEAD_FOLDED = 4
FOLDED = [0, 5, 4]
SUMMED = [2, 2, 0]
PATH_AT = [0, 2, 3, 5]
LAST_HALF = (H - CHUNKS * LAST_ROWS[-1]) // 2
BANK = 512
GATE_CHUNK = 392
GATE_HALF = 4
PAD = W

E_GATE1 = 0
E_GATE2 = E_GATE1 + NF
E_CHAN = E_GATE2 + NF
E_GATE = E_CHAN + 5
E_HID = E_GATE + 6
E_END = E_HID + 4

N_ONES = 0
N_SHIFT = N_ONES + NF
N_TRI = N_SHIFT + 2 * NF
N_EDGE = N_TRI + NF
N_CHAN = N_EDGE + 2
N_BASIS = N_CHAN + PER * P
N_TAP = N_BASIS + CELLS
N_END = N_TAP + TAPS * C

W_BIAS = 0
W_MIX = W_BIAS + PER
W_HIDE = W_MIX + PER * C
W_IDENT = W_HIDE + HID
W_IMAGE = W_IDENT + P
W_PICK = W_IMAGE + GROUP
W_SPREAD = W_PICK + (2 * PER - 1) * QUAD
W_END = W_SPREAD + PER * P


def chunk_rows(turn, s):
    if isinstance(turn, int) and SLOTS * turn + s == 0:
        return HEAD_ROWS
    if isinstance(turn, int) and SLOTS * turn + s == NGROUP - 1:
        return LAST_ROWS
    return CHUNK_ROWS


def vector_rows(rows):
    return H - CHUNKS * rows


def tap_windows(row0, rows, tap):
    if tap == 3:
        return slice(row0 + 1, row0 + 1 + rows), slice(0, W - 1), slice(1, W)
    if tap == 0:
        return slice(row0, row0 + rows), slice(0, W - 1), slice(1, W)
    if tap == 2:
        return slice(row0, row0 + rows), slice(1, W), slice(0, W - 1)
    return slice(row0, row0 + rows), slice(0, W), slice(0, W)


def build(nc, x, early, narrow, wide, out):
    fp32 = mybir.dt.float32
    ALU = mybir.AluOpType
    ACT = mybir.ActivationFunctionType
    AX = mybir.AxisListType

    x_tiles = x.rearrange("n c h w -> (n c) (h w)").rearrange("(g p t) f -> g t p f", p=P, t=PER)
    out_tiles = out.rearrange("n c h w -> (n c) (h w)").rearrange("(g p t) f -> g t p f", p=P, t=PER)
    x_image0 = x[0, :, :, :].rearrange("c h w -> c (h w)")

    with ExitStack() as ctx:
        def sb(name, shape):
            return ctx.enter_context(nc.sbuf_tensor(name, shape, fp32))

        def sem(name):
            return ctx.enter_context(nc.semaphore(name))

        xin = sb("xin", [P, SLOTS, PER, PAD + HW])
        xout = sb("xout", [P, SLOTS, PER, HW])
        ea = sb("ea", [C, E_END])
        na = sb("na", [NF, N_END])
        wi = sb("wi", [P, W_END])
        half_sums = sb("half_sums", [P, 2, DCT, BLK * W // 2])
        pixels = sb("pixels", [P, 2, max(SUMMED) * DCT, BLK, BLK])
        zeros = sb("zeros", [C, GATE_CHUNK])
        filt = sb("filt", [P, PER, CELLS])
        pooled = sb("pooled", [P, PER, 2, CELLS])
        sums = sb("sums", [P, PER, 2])
        by_image = sb("by_image", [P, PER, 2, GROUP])
        mixed = sb("mixed", [C, GROUP])
        gain = sb("gain", [C, GROUP])
        total = sb("total", [C, GROUP])
        hidden = sb("hidden", [HID, GROUP])
        taps = sb("taps", [C, TAPS, GROUP])
        spread = sb("spread", [P, PER * TAPS, GROUP])
        coef = sb("coef", [P, SLOTS, PER, TAPS])
        diag = sb("diag", [P, PER, TAPS, P])
        expo = sb("expo", [C, 1])
        rs_chan = sb("rs_chan", [C, 1])
        rs_gate = sb("rs_gate", [NF, 1])
        rs_hid = sb("rs_hid", [HID, 1])
        a_chan = sb("a_chan", [C, 1])
        b_chan = sb("b_chan", [C, 1])
        a_gate = sb("a_gate", [NF, 1])
        b_gate = sb("b_gate", [NF, 1])
        a_hid = sb("a_hid", [HID, 1])
        b_hid = sb("b_hid", [HID, 1])
        gate_sum = sb("gate_sum", [NF, 2])
        gate_act = sb("gate_act", [NF, 1])
        xg = sb("xg", [NF, 1])
        inv_s = sb("inv_s", [NF, 1])
        share = sb("share", [NF, 1])
        count = sb("count", [NF, 1])
        bounds = sb("bounds", [NF, 2])
        above = sb("above", [NF, PER * P])
        hit = sb("hit", [NF, PER * P])
        chosen = sb("chosen", [NF, PER, P])

        w_gate1 = ea[:, E_GATE1:E_GATE2]
        w_gate2 = ea[0:NF, E_GATE2:E_CHAN]
        chan_par = ea[:, E_CHAN:E_GATE]
        gate_par = ea[0:NF, E_GATE:E_HID]
        hid_par = ea[0:HID, E_HID:E_END]
        ones = na[:, N_ONES:N_SHIFT]
        shift = na[:, N_SHIFT:N_TRI].rearrange("p (a b) -> p a b", a=2)
        tri = na[:, N_TRI:N_EDGE]
        edge = na[:, N_EDGE:N_CHAN]
        chan = na[:, N_CHAN:N_BASIS]
        basis = na[:, N_BASIS:N_TAP]
        w_tap = na[:, N_TAP:N_END].rearrange("p (k c) -> p k c", k=TAPS)
        bias = wi[:, W_BIAS:W_MIX]
        w_mix = wi[:, W_MIX:W_HIDE].rearrange("p (t c) -> p t c", t=PER)
        w_hid = wi[0:C, W_HIDE:W_IDENT]
        ident = wi[:, W_IDENT:W_IMAGE]
        image_of = wi[:, W_IMAGE:W_PICK]
        pick = [wi[:, W_PICK + (PER - 1 - t) * QUAD:W_PICK + (PER - 1 - t) * QUAD + C] for t in range(PER)]
        to_rows = wi[0:C, W_SPREAD:W_END].rearrange("p (t r) -> p t r", t=PER)
        image0 = xout[0:C, SLOTS - 1, PER - 1, :]

        banks = ctx.enter_context(nc.psum_tensor("banks", [P, 8, BANK], fp32))
        p_mixed = banks[0:C, 6, 0:GROUP]
        p_total = banks[0:C, 7, 4:4 + GROUP]
        p_hidden = banks[0:HID, 6, 8:8 + GROUP]
        p_taps = banks[0:C, 6, 16:16 + TAPS * GROUP].rearrange("p (k n) -> p k n", k=TAPS)
        p_spread = banks[:, 6, 32:32 + PER * TAPS * GROUP].rearrange("p (a n) -> p a n", n=GROUP)
        p_gate2 = banks[0:NF, 7, 0:1]
        p_s = banks[0:NF, 7, 1:2]
        p_bounds = banks[0:NF, 7, 2:4]
        p_later = banks[0:NF, 7, 8:8 + PER * P]
        p_filt = banks[:, 6, 0:PER * CELLS]

        def grid(slot, t):
            return xin[:, slot, t, :].rearrange("p (r c) -> p r c", c=W)

        early_halves = xout[:, 1, 0, 0:HEAD_FOLDED * BLK * W // 2].rearrange("p (a f) -> p a f", a=HEAD_FOLDED)
        early_pixels = xout[:, 1, 1, 0:(DCT - HEAD_FOLDED) * DCT * BLK * BLK].rearrange(
            "p (n b d) -> p n b d", b=BLK, d=BLK)

        def result(slot, t):
            return xout[:, slot, t, :].rearrange("p (r c) -> p r c", c=W)

        early_in = sem("early_in")
        narrow_in = sem("narrow_in")
        wide_in = sem("wide_in")
        image0_in = [sem(f"image0_in_{i}") for i in range(4)]
        part_in = sem("part_in")
        zeroed = sem("zeroed")
        loaded = [[sem(f"loaded_{s}_{t}") for t in range(PER)] for s in range(SLOTS)]
        stored = [[sem(f"stored_{s}_{t}") for t in range(PER)] for s in range(SLOTS)]
        pad_zeroed = sem("pad_zeroed")
        halves_done = sem("halves_done")
        expo_set = sem("expo_set")
        rsqrt_done = sem("rsqrt_done")
        fold = sem("fold")
        folded = sem("folded")
        gate_mm = sem("gate_mm")
        gate_relu = sem("gate_relu")
        gate2_mm = sem("gate2_mm")
        gate_tanh = sem("gate_tanh")
        xg_done = sem("xg_done")
        s_mm = sem("s_mm")
        assign = sem("assign")
        counted = sem("counted")
        bounds_mm = sem("bounds_mm")
        hit_done = sem("hit_done")
        later_mm = sem("later_mm")
        chosen_done = sem("chosen_done")
        filt_mm = sem("filt_mm")
        filt_done = sem("filt_done")
        cells_done = sem("cells_done")
        act_cells = sem("act_cells")
        chain = sem("chain")
        sums_done = sem("sums_done")
        mixed_mm = sem("mixed_mm")
        total_mm = sem("total_mm")
        total_done = sem("total_done")
        hidden_mm = sem("hidden_mm")
        hidden_done = sem("hidden_done")
        taps_mm = sem("taps_mm")
        gained_done = sem("gained_done")
        spread_mm = sem("spread_mm")
        coef_done = sem("coef_done")
        diag_done = sem("diag_done")
        own_tap = sem("own_tap")
        first_tap = sem("first_tap")
        tap0_done = sem("tap0_done")
        tap2_done = sem("tap2_done")
        half_tap0_done = sem("half_tap0_done")
        half_tap2_done = sem("half_tap2_done")
        rows_done = sem("rows_done")
        half_rows_done = sem("half_rows_done")
        conv_mm = sem("conv_mm")
        conv_out = sem("conv_out")

        block = ctx.enter_context(nc.Block())

        @block.sync
        def _(sp):
            sp.dma_start(ea[:, :], early).then_inc(early_in, 16)
            quarter = HW // 4
            for i in range(4):
                sp.dma_start(image0[:, quarter * i:quarter * (i + 1)],
                             x_image0[:, quarter * i:quarter * (i + 1)]).then_inc(image0_in[i], 16)
            sp.dma_start(na[:, :], narrow).then_inc(narrow_in, 16)
            for t in range(PER - 1):
                sp.dma_start(xin[:, 0, t, PAD:], x_tiles[0, t]).then_inc(loaded[0][t], 16)
            part = HEAD_FOLDED * BLK * W
            sp.dma_start(xin[:, 0, PER - 1, PAD:PAD + part], x_tiles[0, PER - 1][:, 0:part]).then_inc(part_in, 16)
            sp.dma_start(xin[:, 0, PER - 1, PAD + part:], x_tiles[0, PER - 1][:, part:]).then_inc(loaded[0][PER - 1], 16)
            sp.dma_start(wi[:, :], wide).then_inc(wide_in, 16)
            for t in range(PER):
                sp.dma_start(xin[:, 1, t, PAD:], x_tiles[1, t]).then_inc(loaded[1][t], 16)

            def exchange(turn, last):
                for s in range(SLOTS):
                    for t in range(PER):
                        if last and s == SLOTS - 1 and t == PER - 1:
                            break
                        sp.wait_ge(rows_done, TILES * turn + PER * s + t + 1)
                        sp.wait_ge(conv_out, TILES * turn + PER * s + t + 1)
                        if not last:
                            sp.dma_start(xin[:, s, t, PAD:], x_tiles[SLOTS * turn + SLOTS + s, t]).then_inc(loaded[s][t], 16)
                        sp.dma_start(out_tiles[SLOTS * turn + s, t], xout[:, s, t, :]).then_inc(stored[s][t], 16)

            with sp.Fori(0, TURNS - 1) as turn:
                exchange(turn, False)
            exchange(TURNS - 1, True)
            s, t = SLOTS - 1, PER - 1
            edges = [0, LAST_HALF * W, vector_rows(LAST_ROWS[t]) * W, HW]
            for part, ready, count in [(0, half_rows_done, 1), (2, conv_out, NGROUP * PER), (1, rows_done, NGROUP * PER)]:
                sp.wait_ge(ready, count)
                sp.dma_start(out_tiles[NGROUP - 1, t][:, edges[part]:edges[part + 1]],
                             xout[:, s, t, edges[part]:edges[part + 1]]).then_inc(stored[s][t], 16)
            for s in range(SLOTS):
                for t in range(PER):
                    parts = 3 if s == SLOTS - 1 and t == PER - 1 else 1
                    sp.wait_ge(stored[s][t], 16 * (TURNS - 1 + parts))

        @block.gpsimd
        def _(pool):
            nc.gpsimd.memset(expo[:, :], -0.5).then_inc(expo_set, 1)
            pool.wait_ge(expo_set, 1)
            pool.wait_ge(fold, 3)
            nc.gpsimd.tensor_tensor(rs_gate[:, :], b_gate[:, :], expo[0:NF, 0:1], ALU.pow).then_inc(rsqrt_done, 1)
            nc.gpsimd.tensor_tensor(rs_chan[:, :], b_chan[:, :], expo[:, :], ALU.pow).then_inc(rsqrt_done, 1)
            nc.gpsimd.tensor_tensor(rs_hid[:, :], b_hid[:, :], expo[0:HID, 0:1], ALU.pow).then_inc(rsqrt_done, 1)

            def fold_tile(slot, t, halves, end, first=0):
                cells = xin[:, slot, t, PAD:].rearrange("p (a h f) -> p a h f", a=DCT, h=2)[:, first:end, :, :]
                nc.gpsimd.tensor_tensor(halves[:, first:end, :], cells[:, :, 0, :], cells[:, :, 1, :],
                                        ALU.add).then_inc(halves_done, 1)

            pool.wait_ge(loaded[0][0], 16)
            fold_tile(0, 0, half_sums[:, 1], DCT)
            pool.wait_ge(loaded[0][1], 16)
            fold_tile(0, 1, half_sums[:, 0], HEAD_FOLDED)
            pool.wait_ge(part_in, 16)
            fold_tile(0, 2, early_halves, HEAD_FOLDED)
            pool.wait_ge(loaded[1][0], 16)
            pool.wait_ge(cells_done, 2)
            fold_tile(1, 0, half_sums[:, 1], DCT, HEAD_FOLDED)
            pool.wait_ge(loaded[1][1], 16)
            fold_tile(1, 1, half_sums[:, 0], FOLDED[1])

            def turn_of(turn, first, last):
                for s in range(SLOTS):
                    if last and s == SLOTS - 1:
                        continue
                    g = SLOTS * turn + s
                    other = (s + 1) % SLOTS
                    loads = turn + 1 + (s + 1) // SLOTS
                    if not (first and s == 0):
                        pool.wait_ge(rows_done, PER * g)
                        pool.wait_ge(loaded[other][1], 16 * loads)
                        pool.wait_ge(cells_done, PER * g + 2)
                        fold_tile(other, 1, half_sums[:, 0], FOLDED[1])
                    pool.wait_ge(rows_done, PER * g + 1)
                    pool.wait_ge(loaded[other][2], 16 * loads)
                    pool.wait_ge(cells_done, PER * g + 4 if first and s == 0 else PER * g + 3)
                    fold_tile(other, 2, half_sums[:, 1], FOLDED[2])

            turn_of(0, True, False)
            with pool.Fori(1, TURNS - 1) as turn:
                turn_of(turn, False, False)
            turn_of(TURNS - 1, False, True)

        @block.vector
        def _(dve):
            vec = nc.vector
            vec.memset(zeros[:, :], 0.0).then_inc(zeroed, 1)
            vec.memset(xin[:, :, :, 0:PAD], 0.0).then_inc(pad_zeroed, 1)
            dve.wait_ge(early_in, 16)
            vec.tensor_scalar(b_gate[:, :], gate_par[:, 3:4], EPS, None, ALU.add).then_inc(fold, 1)
            vec.tensor_scalar(b_chan[:, :], chan_par[:, 4:5], EPS, None, ALU.add).then_inc(fold, 1)
            vec.tensor_scalar(b_hid[:, :], hid_par[:, 3:4], EPS, None, ALU.add).then_inc(fold, 1)
            dve.wait_ge(rsqrt_done, 3)
            vec.tensor_tensor(a_gate[:, :], gate_par[:, 0:1], rs_gate[:, :], ALU.mult).then_inc(fold, 1)
            vec.tensor_tensor(a_chan[:, :], chan_par[:, 2:3], rs_chan[:, :], ALU.mult).then_inc(fold, 1)
            vec.tensor_tensor(b_chan[:, :], chan_par[:, 0:1], chan_par[:, 1:2], ALU.subtract).then_inc(fold, 1)
            vec.tensor_tensor(a_hid[:, :], hid_par[:, 0:1], rs_hid[:, :], ALU.mult).then_inc(fold, 1)
            dve.wait_ge(fold, 7)
            vec.tensor_tensor(b_gate[:, :], gate_par[:, 2:3], a_gate[:, :], ALU.mult).then_inc(fold, 1)
            vec.tensor_tensor(b_chan[:, :], b_chan[:, :], a_chan[:, :], ALU.mult).then_inc(fold, 1)
            vec.tensor_tensor(b_hid[:, :], hid_par[:, 2:3], a_hid[:, :], ALU.mult).then_inc(fold, 1)
            dve.wait_ge(fold, 10)
            vec.tensor_tensor(b_gate[:, :], gate_par[:, 1:2], b_gate[:, :], ALU.subtract).then_inc(folded, 1)
            vec.tensor_tensor(b_chan[:, :], b_chan[:, :], chan_par[:, 3:4], ALU.add).then_inc(folded, 1)
            vec.tensor_tensor(b_hid[:, :], hid_par[:, 1:2], b_hid[:, :], ALU.subtract).then_inc(folded, 1)
            vec.tensor_scalar(a_hid[:, :], a_hid[:, :], 1.0 / HW, None, ALU.mult).then_inc(folded, 1)

            def sum_direct(slot, t, end, first=0):
                return vec.tensor_reduce(pooled[:, t, 1, first * DCT:end * DCT].rearrange("p (a c) -> p a c", c=DCT),
                                         xin[:, slot, t, PAD + first * BLK * W:PAD + end * BLK * W].rearrange(
                                             "p (a b c d) -> p a c b d", b=BLK, c=DCT, d=BLK), AX.XY, ALU.add)

            def sum_folded(folds, t, halves, end, first=0):
                dve.wait_ge(halves_done, folds)
                return vec.tensor_reduce(pooled[:, t, 1, first * DCT:end * DCT].rearrange("p (a c) -> p a c", c=DCT),
                                         halves[:, first:end, :].rearrange(
                                             "p a (b c d) -> p a c b d", c=DCT, d=BLK), AX.XY, ALU.add)

            CHAIN = 5

            def of_image(n):
                return image_of.rearrange("p (a n) -> p a n", a=1).broadcast_to([P, n, GROUP])

            def sum_cells(g):
                dve.wait_ge(cells_done, PER * (g + 1))
                dve.wait_ge(act_cells, 1 if isinstance(g, int) and g == 0 else 2 * g)
                vec.tensor_tensor(pooled[:, :, 0, :], pooled[:, :, 1, :], filt[:, :, :], ALU.mult).then_inc(chain, 1)
                dve.wait_ge(chain, CHAIN * g + 1)
                vec.tensor_reduce(sums[:, :, :], pooled[:, :, :, :], AX.X, ALU.add).then_inc(chain, 1)
                dve.wait_ge(chain, CHAIN * g + 2)
                each = sums[:, :, :].rearrange("p t (k n) -> p (t k) n", n=1)
                vec.tensor_tensor(by_image[:, :, :, :].rearrange("p t k n -> p (t k) n"),
                                  each.broadcast_to([P, 2 * PER, GROUP]), of_image(2 * PER), ALU.mult).then_inc(sums_done, 1)

            def gain_steps(g):
                dve.wait_ge(mixed_mm, g + 1)
                vec.tensor_scalar(mixed[:, :], p_mixed, a_chan[:, :], b_chan[:, :], ALU.mult, ALU.add).then_inc(chain, 1)
                dve.wait_ge(chain, CHAIN * g + 3)
                vec.tensor_scalar(gain[:, :], mixed[:, :], 0.0, 1.0, ALU.max, ALU.add).then_inc(chain, 1)
                dve.wait_ge(chain, CHAIN * g + 4)
                dve.wait_ge(total_mm, g + 1)
                vec.tensor_tensor(total[:, :], gain[:, :], p_total, ALU.mult).then_inc(total_done, 1)

            def gained_step(g):
                dve.wait_ge(taps_mm, g + 1)
                vec.tensor_tensor(taps[:, :, :], p_taps,
                                  gain[:, :].rearrange("p (k n) -> p k n", k=1).broadcast_to([C, TAPS, GROUP]),
                                  ALU.mult).then_inc(gained_done, 1)

            def coef_steps(g, slot):
                dve.wait_ge(spread_mm, g + 1)
                vec.tensor_tensor(spread[:, :, :], p_spread, of_image(PER * TAPS), ALU.mult).then_inc(chain, 1)
                dve.wait_ge(chain, CHAIN * g + 5)
                vec.tensor_reduce(coef[:, slot, :, :].rearrange("p t k -> p (t k)"), spread[:, :, :],
                                  AX.X, ALU.add).then_inc(coef_done, 1)

            def tap(slot, t, which, n_rows):
                rows, cols, ocols = tap_windows(0, n_rows, which)
                acc = result(slot, t)[:, 0:n_rows, ocols]
                return vec.scalar_tensor_tensor(out=acc, in0=grid(slot, t)[:, rows, cols],
                                                scalar=coef[:, slot, t, which:which + 1],
                                                in1=acc, op0=ALU.mult, op1=ALU.add)

            dve.wait_ge(gate_tanh, 1)
            vec.tensor_scalar(xg[:, :], gate_act[:, :], 0.0, gate_par[:, 5:6], ALU.max, ALU.add).then_inc(xg_done, 1)
            dve.wait_ge(s_mm, 1)
            vec.reciprocal(inv_s[:, :], p_s).then_inc(assign, 1)
            dve.wait_ge(assign, 1)
            vec.tensor_scalar(share[:, :], xg[:, :], inv_s[:, 0:1], float(C), ALU.mult, ALU.mult).then_inc(assign, 1)
            dve.wait_ge(assign, 2)
            vec.tensor_scalar(count[:, :], share[:, :], ROUND, -ROUND, ALU.add, ALU.add).then_inc(counted, 1)
            dve.wait_ge(narrow_in, 16)
            dve.wait_ge(bounds_mm, 1)
            vec.tensor_tensor(bounds[:, :], p_bounds, edge, ALU.add).then_inc(assign, 1)
            dve.wait_ge(assign, 3)
            vec.tensor_scalar(above[:, :], chan, bounds[:, 0:1], None, ALU.is_ge).then_inc(assign, 1)
            dve.wait_ge(assign, 4)
            vec.scalar_tensor_tensor(out=hit[:, :], in0=chan, scalar=bounds[:, 1:2], in1=above[:, :],
                                     op0=ALU.is_lt, op1=ALU.mult).then_inc(hit_done, 1)
            sum_folded(1, 0, half_sums[:, 1], DCT).then_inc(cells_done, 1)
            dve.wait_ge(later_mm, 1)
            vec.scalar_tensor_tensor(out=chosen[:, :, :].rearrange("p t r -> p (t r)"), in0=p_later, scalar=0.5,
                                     in1=hit[:, :], op0=ALU.is_lt, op1=ALU.mult).then_inc(chosen_done, 1)
            sum_folded(2, 1, half_sums[:, 0], HEAD_FOLDED).then_inc(cells_done, 1)
            sum_folded(3, 2, early_halves, HEAD_FOLDED)
            dve.wait_ge(loaded[0][2], 16)
            sum_direct(0, 2, DCT, HEAD_FOLDED).then_inc(cells_done, 1)
            dve.wait_ge(filt_done, 1)
            dve.wait_ge(wide_in, 16)
            sum_cells(0)
            dve.wait_ge(folded, 4)
            gain_steps(0)
            dve.wait_ge(loaded[1][0], 16)
            sum_direct(1, 0, HEAD_FOLDED)
            gained_step(0)
            sum_folded(4, 0, half_sums[:, 1], DCT, HEAD_FOLDED).then_inc(cells_done, 1)
            coef_steps(0, 0)
            n_pixels = vector_rows(HEAD_ROWS[0]) * W
            dve.wait_ge(coef_done, 1)
            dve.wait_ge(pad_zeroed, 1)
            vec.tensor_scalar(xout[:, 0, 0, 0:n_pixels], xin[:, 0, 0, 0:n_pixels],
                              coef[:, 0, 0, WHOLE_TAP:WHOLE_TAP + 1], bias[:, 0:1], ALU.mult, ALU.add).then_inc(own_tap, 1)

            def tap(turn, s, t, which, first=0, end=None):
                tile = TILES * turn + PER * s + t
                if which == 0:
                    if isinstance(tile, int) and tile == 0:
                        dve.wait_ge(own_tap, 1)
                    else:
                        dve.wait_ge(first_tap, tile)
                elif which == 2:
                    dve.wait_ge(tap0_done, tile + 1)
                else:
                    dve.wait_ge(tap2_done, tile + 1)
                if end is None:
                    end = vector_rows(chunk_rows(turn, s)[t])
                irows, cols, ocols = tap_windows(first, end - first, which)
                acc = result(s, t)[:, first:end, ocols]
                ins = vec.scalar_tensor_tensor(out=acc, in0=grid(s, t)[:, irows, cols],
                                               scalar=coef[:, s, t, which:which + 1],
                                               in1=acc, op0=ALU.mult, op1=ALU.add)
                if isinstance(tile, int) and tile == NGROUP * PER - 1 and first == 0:
                    ins.then_inc({0: half_tap0_done, 2: half_tap2_done, 3: half_rows_done}[which], 1)
                else:
                    ins.then_inc({0: tap0_done, 2: tap2_done, 3: rows_done}[which], 1)

            def turn_of(turn, last):
                for s in range(SLOTS):
                    g = SLOTS * turn + s
                    other = (s + 1) % SLOTS
                    loads = turn + 1 + (s + 1) // SLOTS
                    if last and s == SLOTS - 1:
                        for t in range(PER - 1):
                            for which in (0, 2, 3):
                                tap(turn, s, t, which)
                        for which in (0, 2, 3):
                            tap(turn, s, PER - 1, which, 0, LAST_HALF)
                            tap(turn, s, PER - 1, which, LAST_HALF)
                        continue
                    if isinstance(turn, int) and g == 0:
                        order = [(0, 0), (0, 2), (0, 3), (1, 0), (1, 2)]
                    else:
                        order = [(0, 0), (1, 0), (0, 2), (1, 2), (0, 3)]
                    for t, which in order:
                        tap(turn, s, t, which)
                    sum_folded(2 * g + 5, 1, half_sums[:, 0], FOLDED[1]).then_inc(cells_done, 1)
                    dve.wait_ge(loaded[other][2], 16 * loads)
                    sum_direct(other, 2, DCT, FOLDED[2])
                    sum_folded(2 * g + 6, 2, half_sums[:, 1], FOLDED[2]).then_inc(cells_done, 1)
                    sum_cells(g + 1)
                    tap(turn, s, 1, 3)
                    gain_steps(g + 1)
                    tap(turn, s, 2, 0)
                    gained_step(g + 1)
                    tap(turn, s, 2, 2)
                    coef_steps(g + 1, other)
                    tap(turn, s, 2, 3)
                    if not last:
                        dve.wait_ge(loaded[s][0], 16 * (turn + 2))
                        sum_direct(s, 0, DCT - SUMMED[0]).then_inc(cells_done, 1)

            turn_of(0, False)
            with dve.Fori(1, TURNS - 1) as turn:
                turn_of(turn, False)
            turn_of(TURNS - 1, True)

        @block.scalar
        def _(act):
            sca = nc.scalar
            def sum_cells(loads, slot, t, rows, copies):
                act.wait_ge(loaded[slot][t], 16 * loads)
                cells = xin[:, slot, t, PAD:].rearrange("p (a b c d) -> p a c b d", a=DCT, b=BLK, c=DCT)
                for cell in range(DCT * (DCT - rows), CELLS):
                    ins = sca.activation(copies[:, CELLS - 1 - cell, :, :], cells[:, cell // DCT, cell % DCT, :, :],
                                         ACT.Copy, accum_out=pooled[:, t, 1, cell:cell + 1])
                ins.then_inc(act_cells, 1)

            act.wait_ge(zeroed, 1)
            sca.activation(gate_act[:, :], zeros[0:NF, 0:1], ACT.Tanh)
            for half in range(2):
                if half == 0:
                    act.wait_ge(folded, 1)
                act.wait_ge(gate_mm, half + 1)
                sca.activation(banks[0:NF, GATE_HALF * half:GATE_HALF * (half + 1), 0:GATE_CHUNK],
                               banks[0:NF, GATE_HALF * half:GATE_HALF * (half + 1), 0:GATE_CHUNK], ACT.Relu,
                               bias=b_gate[:, :], scale=a_gate[:, :],
                               accum_out=gate_sum[:, half:half + 1]).then_inc(gate_relu, 1)
            act.wait_ge(gate2_mm, 1)
            sca.activation(gate_act[:, :], p_gate2, ACT.Tanh, bias=gate_par[:, 4:5],
                           scale=1.0 / HW).then_inc(gate_tanh, 1)
            sum_cells(1, 0, 1, DCT - HEAD_FOLDED, early_pixels)
            act.wait_ge(filt_mm, 1)
            sca.activation(filt[:, :, :].rearrange("p t c -> p (t c)"), p_filt, ACT.Copy).then_inc(filt_done, 1)

            def hidden_relu(g):
                act.wait_ge(hidden_mm, g + 1)
                sca.activation(hidden[:, :], p_hidden, ACT.Relu, bias=b_hid[:, :],
                               scale=a_hid[:, :]).then_inc(hidden_done, 1)

            def diagonals(turn, s, t):
                act.wait_ge(coef_done, SLOTS * turn + s + 1)
                for w in range(TAPS):
                    ins = sca.activation(diag[:, t, w, :], ident, ACT.Copy, scale=coef[:, s, t, w:w + 1])
                ins.then_inc(diag_done, 1)

            def tap_and_bias(turn, s, t):
                n_rows = vector_rows(chunk_rows(turn, s)[t])
                if not (isinstance(turn, int) and turn == 0):
                    act.wait_ge(stored[s][t], 16 * turn)
                sca.activation(xout[:, s, t, 0:n_rows * W], xin[:, s, t, 0:n_rows * W], ACT.Identity,
                               bias=bias[:, t:t + 1],
                               scale=coef[:, s, t, WHOLE_TAP:WHOLE_TAP + 1]).then_inc(first_tap, 1)

            def start_tile(turn, s, t):
                diagonals(turn, s, t)
                tap_and_bias(turn, s, t)

            def take_psum(turn, s, t):
                act.wait_ge(conv_mm, TILES * turn + PER * s + t + 1)
                rows = chunk_rows(turn, s)
                first = CHUNKS * ((PER * s + t) % 2)
                sca.activation(xout[:, s, t, vector_rows(rows[t]) * W:].rearrange("p (b f) -> p b f", b=CHUNKS),
                               banks[:, first:first + CHUNKS, 0:rows[t] * W], ACT.Identity,
                               bias=bias[:, t:t + 1]).then_inc(conv_out, 1)

            act.wait_ge(folded, 4)
            hidden_relu(0)
            act.wait_ge(pad_zeroed, 1)
            act.wait_ge(wide_in, 16)
            diagonals(0, 0, 0)

            def turn_of(turn, last):
                for s in range(SLOTS):
                    final = last and s == SLOTS - 1
                    after = (turn + (s + 1) // SLOTS, (s + 1) % SLOTS)
                    if isinstance(turn, int) and SLOTS * turn + s == 0:
                        tap_and_bias(turn, s, 1)
                    diagonals(turn, s, 1)
                    if not final:
                        sum_cells(after[0] + 1, after[1], 1, SUMMED[1], pixels[:, 1])
                    take_psum(turn, s, 0)
                    start_tile(turn, s, 2)
                    take_psum(turn, s, 1)
                    if not final:
                        hidden_relu(SLOTS * turn + s + 1)
                        if not last:
                            sum_cells(turn + 2, s, 0, SUMMED[0], pixels[:, 0])
                        start_tile(*after, 0)
                    take_psum(turn, s, 2)
                    if not final:
                        tap_and_bias(*after, 1)

            turn_of(0, False)
            with act.Fori(1, TURNS - 1) as turn:
                turn_of(turn, False)
            turn_of(TURNS - 1, True)

        @block.tensor
        def _(pe):
            mm = nc.tensor.matmul
            def warm(products, columns=GATE_CHUNK):
                for _ in range(products):
                    mm(banks[:, 0, 0:columns], zeros[:, 0:P], zeros[:, 0:columns], start=True, stop=True)

            pe.wait_ge(zeroed, 1)
            warm(3)
            pe.wait_ge(early_in, 16)
            for half in range(2):
                for b in range(GATE_HALF * half, GATE_HALF * (half + 1)):
                    if b % 2 == 0:
                        pe.wait_ge(image0_in[b // 2], 16)
                    ins = mm(banks[0:NF, b, 0:GATE_CHUNK], w_gate1,
                             image0[:, GATE_CHUNK * b:GATE_CHUNK * (b + 1)], start=True, stop=True)
                ins.then_inc(gate_mm, 1)
            pe.wait_ge(gate_relu, 2)
            for half in range(2):
                ins = mm(p_gate2, w_gate2, gate_sum[:, half:half + 1], start=(half == 0), stop=(half == 1))
            ins.then_inc(gate2_mm, 1)
            pe.wait_ge(narrow_in, 16)
            pe.wait_ge(xg_done, 1)
            mm(p_s, ones, xg[:, :], start=True, stop=True).then_inc(s_mm, 1)
            pe.wait_ge(counted, 1)
            for b in range(2):
                ins = mm(p_bounds[:, b:b + 1], shift[:, b, :], count[:, :], start=True, stop=True)
            ins.then_inc(bounds_mm, 1)
            pe.wait_ge(hit_done, 1)
            mm(p_later, tri, hit[:, :], start=True, stop=True).then_inc(later_mm, 1)
            pe.wait_ge(chosen_done, 1)
            for t in range(PER):
                ins = mm(p_filt[:, CELLS * t:CELLS * (t + 1)], chosen[:, t, :], basis, start=True, stop=True)
            ins.then_inc(filt_mm, 1)

            def mix(g):
                pe.wait_ge(sums_done, g + 1)
                for t in range(PER):
                    ins = mm(p_mixed, w_mix[:, t, :], by_image[:, t, 0, :], start=(t == 0), stop=(t == PER - 1))
                ins.then_inc(mixed_mm, 1)
                for t in range(PER):
                    ins = mm(p_total, pick[t], by_image[:, t, 1, :], start=(t == 0), stop=(t == PER - 1))
                ins.then_inc(total_mm, 1)

            def hide(g):
                pe.wait_ge(total_done, g + 1)
                mm(p_hidden, w_hid, total[:, :], start=True, stop=True).then_inc(hidden_mm, 1)

            def make_taps(g):
                pe.wait_ge(hidden_done, g + 1)
                for w in range(TAPS):
                    ins = mm(p_taps[:, w, :], w_tap[:, w, :], hidden[:, :], start=True, stop=True)
                ins.then_inc(taps_mm, 1)

            def spread_taps(g):
                pe.wait_ge(gained_done, g + 1)
                for t in range(PER):
                    ins = mm(p_spread[:, TAPS * t:TAPS * (t + 1), :], to_rows[:, t, :], taps[:, :, :],
                             start=True, stop=True)
                ins.then_inc(spread_mm, 1)

            def conv_tap(rows, s, t, chunk, which):
                n = rows[t]
                bank = CHUNKS * ((PER * s + t) % 2) + chunk
                r, cols, ocols = tap_windows(vector_rows(n) + n * chunk, n, which)
                acc = banks[:, bank, 0:n * W].rearrange("p (r c) -> p r c", c=W)
                return mm(acc[:, :, ocols], diag[:, t, which, :], grid(s, t)[:, r, cols],
                          start=(which == WHOLE_TAP), stop=(which == 3))

            TAP_ORDER = [WHOLE_TAP, 0, 2, 3]

            def conv_start(turn, s, t):
                pe.wait_ge(diag_done, TILES * turn + PER * s + t + 1)
                tile = TILES * turn + PER * s + t
                if isinstance(tile, int) and tile < 2:
                    return
                pe.wait_ge(conv_out, tile - 1)

            def conv(turn, s, t, between=()):
                between = dict(between)
                conv_start(turn, s, t)
                for n in range(CHUNKS * TAPS):
                    if n in between:
                        between[n]()
                    ins = conv_tap(chunk_rows(turn, s), s, t, n // TAPS, TAP_ORDER[n % TAPS])
                ins.then_inc(conv_mm, 1)

            warm(3)
            pe.wait_ge(wide_in, 16)
            mix(0)
            hide(0)
            warm(1, 256)
            make_taps(0)
            warm(1, 256)
            spread_taps(0)
            warm(1)

            def turn_of(turn, last):
                for s in range(SLOTS):
                    if last and s == SLOTS - 1:
                        for t in range(PER):
                            conv(turn, s, t)
                        continue
                    g = SLOTS * turn + s
                    conv(turn, s, 0)
                    conv(turn, s, 1)
                    conv(turn, s, 2, zip(PATH_AT, [lambda: mix(g + 1), lambda: hide(g + 1),
                                                               lambda: make_taps(g + 1), lambda: spread_taps(g + 1)]))

            turn_of(0, False)
            with pe.Fori(1, TURNS - 1) as turn:
                turn_of(turn, False)
            turn_of(TURNS - 1, True)


def constants():
    import numpy as np
    low_x = [0, 0, 1, 1, 0, 2, 2, 1, 2, 0, 3, 4, 0, 1, 3, 0, 1, 2, 3, 4, 5, 0, 1, 2, 3, 4, 5, 6, 1, 2, 3, 4]
    low_y = [0, 1, 0, 1, 2, 0, 1, 2, 2, 3, 0, 0, 4, 3, 1, 5, 4, 3, 2, 1, 0, 6, 5, 4, 3, 2, 1, 0, 6, 5, 4, 3]

    def wave(freq):
        f = np.array(freq, np.float64)[:, None]
        r = np.cos(np.pi * f * (np.arange(DCT)[None, :] + 0.5) / DCT) / np.sqrt(DCT)
        return np.where(f == 0, r, r * np.sqrt(2.0))

    k = np.zeros((NF, N_END), np.float32)
    k[:, N_ONES:N_SHIFT] = 1.0
    low, high = np.zeros((NF, NF)), np.zeros((NF, NF))
    for i in range(NF - 1):
        low[i, i + 1] = 1.0
        high[i, i] = 1.0
        high[i, NF - 1] = -1.0
    k[:, N_SHIFT:N_SHIFT + NF] = low
    k[:, N_SHIFT + NF:N_TRI] = high
    k[NF - 1, N_EDGE + 1] = C
    k[:, N_TRI:N_EDGE] = np.tril(np.ones((NF, NF)), -1)
    rows = np.arange(P)
    for t in range(PER):
        k[:, N_CHAN + P * t:N_CHAN + P * (t + 1)] = PER * (rows % QUAD) + t
    basis = wave(low_x)[:, :, None] * wave(low_y)[:, None, :]
    k[:, N_BASIS:N_TAP] = basis.reshape(NF, CELLS) / (BLK * BLK)

    w = np.zeros((P, W_END), np.float32)
    w[:, W_IDENT:W_IMAGE] = np.eye(P)
    w[:, W_IMAGE:W_PICK] = rows[:, None] // QUAD == np.arange(GROUP)
    w[:, W_PICK + (PER - 1) * QUAD:][:, :QUAD] = rows[:, None] % QUAD == np.arange(QUAD)
    for t in range(PER):
        w[QUAD * t:QUAD * (t + 1), W_SPREAD + P * t:W_SPREAD + P * (t + 1)] = np.arange(QUAD)[:, None] == rows % QUAD
    return k, w


def kernel(x, L0_conv_wg1, L0_conv_bn2_g, L0_conv_bn2_b, L0_conv_bn2_m, L0_conv_bn2_v, L0_conv_wg2,
           L0_conv_bg2, L0_conv_beta, L0_conv_w1d, L0_conv_b1d, L0_conv_bn1_g, L0_conv_bn1_b, L0_conv_bn1_m,
           L0_conv_bn1_v, L1_conv_w1, L1_conv_gamma, L1_conv_beta, L1_conv_running_mean,
           L1_conv_running_var, L1_conv_w2, L1_conv_b2, L1_conv_bias):
    import numpy as np
    import concourse.bacc as bacc
    from concourse.bass_utils import run_bass_kernel_spmd as run

    a = np.asarray
    by_tile = lambda v: v.reshape((QUAD, PER) + v.shape[1:]).swapaxes(0, 1).reshape(v.shape)
    narrow, wide = constants()
    early = np.zeros((C, E_END), np.float32)
    early[:, E_GATE1:E_GATE2] = a(L0_conv_wg1).T
    early[:NF, E_GATE2:E_CHAN] = a(L0_conv_wg2).T
    early[:, E_CHAN:E_GATE] = by_tile(np.stack([a(L0_conv_b1d), a(L0_conv_bn1_m), a(L0_conv_bn1_g),
                                                a(L0_conv_bn1_b), a(L0_conv_bn1_v)], axis=1))
    early[:NF, E_GATE:E_HID] = np.stack([a(L0_conv_bn2_g), a(L0_conv_bn2_b), a(L0_conv_bn2_m), a(L0_conv_bn2_v),
                                         a(L0_conv_bg2), np.repeat(a(L0_conv_beta), NF)], axis=1)
    early[:RED, E_HID:E_END] = np.stack([a(L1_conv_gamma), a(L1_conv_beta), a(L1_conv_running_mean),
                                         a(L1_conv_running_var)], axis=1)
    early[RED:HID, E_END - 1] = 1.0
    early[RED, E_HID + 1] = 1.0
    make = np.zeros((HID, TAPS, C), np.float32)
    make[:RED] = by_tile(a(L1_conv_w2).reshape(C, 9, RED)).transpose(2, 1, 0)[:, :TAPS]
    make[RED] = by_tile(a(L1_conv_b2).reshape(C, 9)).T[:TAPS]
    narrow[:, N_TAP:N_END] = make.reshape(HID, TAPS * C)
    mix = by_tile(a(L0_conv_w1d)[:, :, 1]).T.reshape(QUAD, PER * C)
    wide[:, W_BIAS:W_MIX] = np.tile(a(L1_conv_bias).reshape(QUAD, PER), (GROUP, 1))
    wide[:, W_MIX:W_HIDE] = np.tile(mix, (GROUP, 1))
    wide[:C, W_HIDE:W_HIDE + RED] = by_tile(a(L1_conv_w1).T)
    arrays = {"x": a(x), "early": early, "narrow": narrow, "wide": wide}
    arrays = {name: np.ascontiguousarray(v) for name, v in arrays.items()}
    nc = bacc.Bacc("TRN2", target_bir_lowering=False, num_devices=1)
    args = [nc.dram_tensor(name, v.shape, mybir.dt.float32, kind="ExternalInput").ap() for name, v in arrays.items()]
    out = nc.dram_tensor("out", (NIMG, C, H, W), mybir.dt.float32, kind="ExternalOutput").ap()
    build(nc, *args, out)
    r = run(nc, [arrays], core_ids=[0])
    return r.results[0]["out"]
```

```python
from contextlib import ExitStack

import concourse.bass as bass
from concourse import mybir

NIMG, C, H, W = 32, 96, 56, 56
HW = H * W
P = 128
QUAD = 32
PER = C // QUAD
GROUP = P // QUAD
NGROUP = NIMG // GROUP
SLOTS = 2
TURNS = NGROUP // SLOTS
TILES = SLOTS * PER
DCT = 7
BLK = H // DCT
CELLS = DCT * DCT
NF = 32
RED = 24
HID = 32
TAPS = 4
WHOLE_TAP = 1
EPS = 1e-05
ROUND = 12582912.0

CHUNKS = 3
CHUNK_ROWS = [7, 7, 7]
HEAD_ROWS = [6, 7, 7]
LAST_ROWS = [6, 6, 6]
LAST_HALF = [None] + [(H - CHUNKS * n) // 2 for n in LAST_ROWS[1:]]
FOLDED = [0, 3, 4]
SUMMED = [2, 4, 0]
HEAD_SUMMED = 5
HEAD_FOLDED = 4
HEAD_PART = 5
HEAD_BEFORE = 2
PATH_AT = [1, 3, 4, 6]
BANK = 512
GATE_CHUNK = 392
GATE_HALF = 4
PAD = W

E_GATE1 = 0
E_GATE2 = E_GATE1 + NF
E_CHAN = E_GATE2 + NF
E_GATE = E_CHAN + 5
E_HID = E_GATE + 6
E_END = E_HID + 4

N_ONES = 0
N_SHIFT = N_ONES + NF
N_TRI = N_SHIFT + 2 * NF
N_EDGE = N_TRI + NF
N_CHAN = N_EDGE + 2
N_BASIS = N_CHAN + PER * P
N_TAP = N_BASIS + CELLS
N_END = N_TAP + TAPS * C

W_BIAS = 0
W_MIX = W_BIAS + PER
W_HIDE = W_MIX + PER * C
W_IDENT = W_HIDE + HID
W_IMAGE = W_IDENT + P
W_PICK = W_IMAGE + GROUP
W_SPREAD = W_PICK + (2 * PER - 1) * QUAD
W_END = W_SPREAD + PER * P


def chunk_rows(turn, s):
    if isinstance(turn, int) and SLOTS * turn + s == 0:
        return HEAD_ROWS
    if isinstance(turn, int) and SLOTS * turn + s == NGROUP - 1:
        return LAST_ROWS
    return CHUNK_ROWS


def vector_rows(rows):
    return H - CHUNKS * rows


def tap_windows(row0, rows, tap):
    if tap == 3:
        return slice(row0 + 1, row0 + 1 + rows), slice(0, W - 1), slice(1, W)
    if tap == 0:
        return slice(row0, row0 + rows), slice(0, W - 1), slice(1, W)
    if tap == 2:
        return slice(row0, row0 + rows), slice(1, W), slice(0, W - 1)
    return slice(row0, row0 + rows), slice(0, W), slice(0, W)


def build(nc, x, early, narrow, wide, out):
    fp32 = mybir.dt.float32
    ALU = mybir.AluOpType
    ACT = mybir.ActivationFunctionType
    AX = mybir.AxisListType

    x_tiles = x.rearrange("n c h w -> (n c) (h w)").rearrange("(g p t) f -> g t p f", p=P, t=PER)
    out_tiles = out.rearrange("n c h w -> (n c) (h w)").rearrange("(g p t) f -> g t p f", p=P, t=PER)
    x_image0 = x[0, :, :, :].rearrange("c h w -> c (h w)")

    with ExitStack() as ctx:
        def sb(name, shape):
            return ctx.enter_context(nc.sbuf_tensor(name, shape, fp32))

        def sem(name):
            return ctx.enter_context(nc.semaphore(name))

        xin = sb("xin", [P, SLOTS, PER, PAD + HW])
        xout = sb("xout", [P, SLOTS, PER, HW])
        early_sb = sb("early_sb", [C, E_END])
        narrow_sb = sb("narrow_sb", [NF, N_END])
        wide_sb = sb("wide_sb", [P, W_END])
        half_sums = sb("half_sums", [P, 2, DCT, BLK * W // 2])
        pixels = sb("pixels", [P, 2, max(SUMMED) * DCT, BLK, BLK])
        zeros = sb("zeros", [P, GATE_CHUNK])
        filt = sb("filt", [P, PER, CELLS])
        pooled = sb("pooled", [P, PER, CELLS])
        weighted = sb("weighted", [P, PER, CELLS])
        sums = sb("sums", [P, PER, 2])
        by_image = sb("by_image", [P, PER, 2, GROUP])
        lift = sb("lift", [C, GROUP])
        total = sb("total", [C, GROUP])
        hidden = sb("hidden", [HID, GROUP])
        taps = sb("taps", [C, TAPS, GROUP])
        spread = sb("spread", [P, PER * TAPS, GROUP])
        coef = sb("coef", [P, SLOTS, PER, TAPS])
        diag = sb("diag", [P, PER, TAPS, P])
        expo = sb("expo", [C, 1])
        rs_chan = sb("rs_chan", [C, 1])
        rs_gate = sb("rs_gate", [NF, 1])
        rs_hid = sb("rs_hid", [HID, 1])
        a_chan = sb("a_chan", [C, 1])
        b_chan = sb("b_chan", [C, 1])
        a_gate = sb("a_gate", [NF, 1])
        b_gate = sb("b_gate", [NF, 1])
        a_hid = sb("a_hid", [HID, 1])
        b_hid = sb("b_hid", [HID, 1])
        gate_sum = sb("gate_sum", [NF, 2])
        gate_act = sb("gate_act", [NF, 1])
        xg = sb("xg", [NF, 1])
        inv_s = sb("inv_s", [NF, 1])
        share = sb("share", [NF, 1])
        count = sb("count", [NF, 1])
        bounds = sb("bounds", [NF, 2])
        above = sb("above", [NF, PER * P])
        hit = sb("hit", [NF, PER * P])
        chosen = sb("chosen", [NF, PER, P])

        w_gate1 = early_sb[:, E_GATE1:E_GATE2]
        w_gate2 = early_sb[0:NF, E_GATE2:E_CHAN]
        chan_par = early_sb[:, E_CHAN:E_GATE]
        gate_par = early_sb[0:NF, E_GATE:E_HID]
        hid_par = early_sb[0:HID, E_HID:E_END]
        ones = narrow_sb[:, N_ONES:N_SHIFT]
        shift = narrow_sb[:, N_SHIFT:N_TRI].rearrange("p (a b) -> p a b", a=2)
        tri = narrow_sb[:, N_TRI:N_EDGE]
        edge = narrow_sb[:, N_EDGE:N_CHAN]
        chan = narrow_sb[:, N_CHAN:N_BASIS]
        basis = narrow_sb[:, N_BASIS:N_TAP]
        w_tap = narrow_sb[:, N_TAP:N_END].rearrange("p (k c) -> p k c", k=TAPS)
        bias = wide_sb[:, W_BIAS:W_MIX]
        w_mix = wide_sb[:, W_MIX:W_HIDE].rearrange("p (t c) -> p t c", t=PER)
        w_hid = wide_sb[0:C, W_HIDE:W_IDENT]
        ident = wide_sb[:, W_IDENT:W_IMAGE]
        image_of = wide_sb[:, W_IMAGE:W_PICK]
        pick = [wide_sb[:, W_PICK + (PER - 1 - t) * QUAD:W_PICK + (PER - 1 - t) * QUAD + C] for t in range(PER)]
        to_rows = wide_sb[0:C, W_SPREAD:W_END].rearrange("p (t r) -> p t r", t=PER)
        image0 = xout[0:C, SLOTS - 1, PER - 1, :]

        banks = ctx.enter_context(nc.psum_tensor("banks", [P, 8, BANK], fp32))
        p_mixed = banks[0:C, 6, 0:GROUP]
        p_total = banks[0:C, 7, 4:4 + GROUP]
        p_hidden = banks[0:HID, 6, 8:8 + GROUP]
        p_taps = banks[0:C, 6, 16:16 + TAPS * GROUP].rearrange("p (k n) -> p k n", k=TAPS)
        p_spread = banks[:, 6, 32:32 + PER * TAPS * GROUP].rearrange("p (a n) -> p a n", n=GROUP)
        p_gate2 = banks[0:NF, 7, 0:1]
        p_s = banks[0:NF, 7, 1:2]
        p_bounds = banks[0:NF, 7, 2:4]
        p_later = banks[0:NF, 7, 8:8 + PER * P]
        p_filt = banks[:, 6, 0:PER * CELLS]

        def grid(slot, t):
            return xin[:, slot, t, :].rearrange("p (r c) -> p r c", c=W)

        early_halves = xout[:, 1, 0, 0:HEAD_FOLDED * BLK * W // 2].rearrange("p (a f) -> p a f", a=HEAD_FOLDED)
        early_pixels = xout[:, 1, 1, 0:(DCT - HEAD_FOLDED) * DCT * BLK * BLK].rearrange(
            "p (n b d) -> p n b d", b=BLK, d=BLK)

        def result(slot, t):
            return xout[:, slot, t, :].rearrange("p (r c) -> p r c", c=W)

        early_in = sem("early_in")
        narrow_in = sem("narrow_in")
        wide_in = sem("wide_in")
        image0_in = [sem(f"image0_in_{i}") for i in range(4)]
        part_in = sem("part_in")
        zeroed = sem("zeroed")
        loaded = [[sem(f"loaded_{s}_{t}") for t in range(PER)] for s in range(SLOTS)]
        stored = [[sem(f"stored_{s}_{t}") for t in range(PER)] for s in range(SLOTS)]
        pad_zeroed = sem("pad_zeroed")
        halves_done = sem("halves_done")
        expo_set = sem("expo_set")
        rsqrt_done = sem("rsqrt_done")
        fold = sem("fold")
        folded = sem("folded")
        gate_mm = sem("gate_mm")
        gate_relu = sem("gate_relu")
        gate2_mm = sem("gate2_mm")
        gate_tanh = sem("gate_tanh")
        xg_done = sem("xg_done")
        s_mm = sem("s_mm")
        assign = sem("assign")
        counted = sem("counted")
        bounds_mm = sem("bounds_mm")
        hit_done = sem("hit_done")
        later_mm = sem("later_mm")
        chosen_done = sem("chosen_done")
        filt_mm = sem("filt_mm")
        filt_done = sem("filt_done")
        cells_done = sem("cells_done")
        act_cells = sem("act_cells")
        chain = sem("chain")
        sums_done = sem("sums_done")
        mixed_mm = sem("mixed_mm")
        total_mm = sem("total_mm")
        lift_done = sem("lift_done")
        total_done = sem("total_done")
        hidden_mm = sem("hidden_mm")
        hidden_done = sem("hidden_done")
        taps_mm = sem("taps_mm")
        gained_done = sem("gained_done")
        spread_mm = sem("spread_mm")
        coef_done = sem("coef_done")
        diag_done = sem("diag_done")
        own_tap = sem("own_tap")
        first_tap = sem("first_tap")
        tap0_done = sem("tap0_done")
        tap2_done = sem("tap2_done")
        half_tap0_done = sem("half_tap0_done")
        half_tap2_done = sem("half_tap2_done")
        rows_done = sem("rows_done")
        half_rows_done = sem("half_rows_done")
        conv_mm = sem("conv_mm")
        conv_out = sem("conv_out")

        block = ctx.enter_context(nc.Block())

        @block.sync
        def _(sp):
            sp.dma_start(early_sb[:, :], early).then_inc(early_in, 16)
            quarter = HW // 4
            for i in range(4):
                sp.dma_start(image0[:, quarter * i:quarter * (i + 1)],
                             x_image0[:, quarter * i:quarter * (i + 1)]).then_inc(image0_in[i], 16)
            sp.dma_start(narrow_sb[:, :], narrow).then_inc(narrow_in, 16)
            for t in range(PER - 1):
                sp.dma_start(xin[:, 0, t, PAD:], x_tiles[0, t]).then_inc(loaded[0][t], 16)
            part = HEAD_PART * BLK * W
            sp.dma_start(xin[:, 0, PER - 1, PAD:PAD + part], x_tiles[0, PER - 1][:, 0:part]).then_inc(part_in, 16)
            sp.dma_start(xin[:, 0, PER - 1, PAD + part:], x_tiles[0, PER - 1][:, part:]).then_inc(loaded[0][PER - 1], 16)
            sp.dma_start(wide_sb[:, :], wide).then_inc(wide_in, 16)
            for t in range(PER):
                sp.dma_start(xin[:, 1, t, PAD:], x_tiles[1, t]).then_inc(loaded[1][t], 16)

            def exchange(turn, last):
                for s in range(SLOTS):
                    for t in range(PER):
                        if last and s == SLOTS - 1 and t > 0:
                            break
                        sp.wait_ge(rows_done, TILES * turn + PER * s + t + 1)
                        sp.wait_ge(conv_out, TILES * turn + PER * s + t + 1)
                        if not last:
                            sp.dma_start(xin[:, s, t, PAD:], x_tiles[SLOTS * turn + SLOTS + s, t]).then_inc(loaded[s][t], 16)
                        sp.dma_start(out_tiles[SLOTS * turn + s, t], xout[:, s, t, :]).then_inc(stored[s][t], 16)

            with sp.Fori(0, TURNS - 1) as turn:
                exchange(turn, False)
            exchange(TURNS - 1, True)
            s = SLOTS - 1
            for t, first, end, waits in [
                    (1, 0, LAST_HALF[1], [(half_rows_done, 1)]),
                    (1, LAST_HALF[1], H, [(rows_done, NGROUP * PER - 1), (conv_out, NGROUP * PER - 1)]),
                    (2, 0, LAST_HALF[2], [(half_rows_done, 2)]),
                    (2, LAST_HALF[2], vector_rows(LAST_ROWS[2]), [(rows_done, NGROUP * PER)]),
                    (2, vector_rows(LAST_ROWS[2]), H, [(conv_out, NGROUP * PER)])]:
                for ready, count in waits:
                    sp.wait_ge(ready, count)
                sp.dma_start(out_tiles[NGROUP - 1, t][:, first * W:end * W],
                             xout[:, s, t, first * W:end * W]).then_inc(stored[s][t], 16)
            for s in range(SLOTS):
                for t in range(PER):
                    parts = t + 1 if s == SLOTS - 1 else 1
                    sp.wait_ge(stored[s][t], 16 * (TURNS - 1 + parts))

        @block.gpsimd
        def _(pool):
            nc.gpsimd.memset(expo[:, :], -0.5).then_inc(expo_set, 1)
            pool.wait_ge(expo_set, 1)
            pool.wait_ge(fold, 3)
            nc.gpsimd.tensor_tensor(rs_gate[:, :], b_gate[:, :], expo[0:NF, 0:1], ALU.pow).then_inc(rsqrt_done, 1)
            nc.gpsimd.tensor_tensor(rs_chan[:, :], b_chan[:, :], expo[:, :], ALU.pow).then_inc(rsqrt_done, 1)
            nc.gpsimd.tensor_tensor(rs_hid[:, :], b_hid[:, :], expo[0:HID, 0:1], ALU.pow).then_inc(rsqrt_done, 1)

            def fold_tile(slot, t, halves, end, first=0):
                cells = xin[:, slot, t, PAD:].rearrange("p (a h f) -> p a h f", a=DCT, h=2)[:, first:end, :, :]
                nc.gpsimd.tensor_tensor(halves[:, first:end, :], cells[:, :, 0, :], cells[:, :, 1, :],
                                        ALU.add).then_inc(halves_done, 1)

            pool.wait_ge(loaded[0][1], 16)
            fold_tile(0, 1, half_sums[:, 0], HEAD_FOLDED)
            pool.wait_ge(part_in, 16)
            fold_tile(0, 2, early_halves, HEAD_FOLDED)
            pool.wait_ge(loaded[1][0], 16)
            pool.wait_ge(cells_done, 2)
            fold_tile(1, 0, half_sums[:, 1], DCT, HEAD_FOLDED)
            pool.wait_ge(loaded[1][1], 16)
            fold_tile(1, 1, half_sums[:, 0], FOLDED[1])

            def turn_of(turn, first, last):
                for s in range(SLOTS):
                    if last and s == SLOTS - 1:
                        continue
                    g = SLOTS * turn + s
                    other = (s + 1) % SLOTS
                    loads = turn + 1 + (s + 1) // SLOTS
                    if not (first and s == 0):
                        pool.wait_ge(rows_done, PER * g)
                        pool.wait_ge(loaded[other][1], 16 * loads)
                        pool.wait_ge(cells_done, PER * g + 2)
                        fold_tile(other, 1, half_sums[:, 0], FOLDED[1])
                    pool.wait_ge(rows_done, PER * g + 1)
                    pool.wait_ge(loaded[other][2], 16 * loads)
                    pool.wait_ge(cells_done, PER * g + 4 if first and s == 0 else PER * g + 3)
                    fold_tile(other, 2, half_sums[:, 1], FOLDED[2])

            turn_of(0, True, False)
            with pool.Fori(1, TURNS - 1) as turn:
                turn_of(turn, False, False)
            turn_of(TURNS - 1, False, True)

        @block.vector
        def _(dve):
            vec = nc.vector
            vec.memset(zeros[:, :], 0.0).then_inc(zeroed, 1)
            vec.memset(xin[:, :, :, 0:PAD], 0.0).then_inc(pad_zeroed, 1)
            dve.wait_ge(early_in, 16)
            vec.tensor_scalar(b_gate[:, :], gate_par[:, 3:4], EPS, None, ALU.add).then_inc(fold, 1)
            vec.tensor_scalar(b_chan[:, :], chan_par[:, 4:5], EPS, None, ALU.add).then_inc(fold, 1)
            vec.tensor_scalar(b_hid[:, :], hid_par[:, 3:4], EPS, None, ALU.add).then_inc(fold, 1)
            dve.wait_ge(rsqrt_done, 3)
            vec.tensor_tensor(a_gate[:, :], gate_par[:, 0:1], rs_gate[:, :], ALU.mult).then_inc(fold, 1)
            vec.tensor_tensor(a_chan[:, :], chan_par[:, 2:3], rs_chan[:, :], ALU.mult).then_inc(fold, 1)
            vec.tensor_tensor(b_chan[:, :], chan_par[:, 0:1], chan_par[:, 1:2], ALU.subtract).then_inc(fold, 1)
            vec.tensor_tensor(a_hid[:, :], hid_par[:, 0:1], rs_hid[:, :], ALU.mult).then_inc(fold, 1)
            dve.wait_ge(fold, 7)
            vec.tensor_tensor(b_gate[:, :], gate_par[:, 2:3], a_gate[:, :], ALU.mult).then_inc(fold, 1)
            vec.tensor_tensor(b_chan[:, :], b_chan[:, :], a_chan[:, :], ALU.mult).then_inc(fold, 1)
            vec.tensor_tensor(b_hid[:, :], hid_par[:, 2:3], a_hid[:, :], ALU.mult).then_inc(fold, 1)
            dve.wait_ge(fold, 10)
            vec.tensor_tensor(b_gate[:, :], gate_par[:, 1:2], b_gate[:, :], ALU.subtract).then_inc(folded, 1)
            vec.tensor_tensor(b_chan[:, :], b_chan[:, :], chan_par[:, 3:4], ALU.add).then_inc(folded, 1)
            vec.tensor_tensor(b_hid[:, :], hid_par[:, 1:2], b_hid[:, :], ALU.subtract).then_inc(folded, 1)
            vec.tensor_scalar(a_hid[:, :], a_hid[:, :], 1.0 / HW, None, ALU.mult).then_inc(folded, 1)

            def sum_direct(slot, t, end, first=0):
                return vec.tensor_reduce(pooled[:, t, first * DCT:end * DCT].rearrange("p (a c) -> p a c", c=DCT),
                                         xin[:, slot, t, PAD + first * BLK * W:PAD + end * BLK * W].rearrange(
                                             "p (a b c d) -> p a c b d", b=BLK, c=DCT, d=BLK), AX.XY, ALU.add)

            def sum_folded(folds, t, halves, end, first=0):
                dve.wait_ge(halves_done, folds)
                return vec.tensor_reduce(pooled[:, t, first * DCT:end * DCT].rearrange("p (a c) -> p a c", c=DCT),
                                         halves[:, first:end, :].rearrange(
                                             "p a (b c d) -> p a c b d", c=DCT, d=BLK), AX.XY, ALU.add)

            CHAIN = 3

            def of_image(n):
                return image_of.rearrange("p (a n) -> p a n", a=1).broadcast_to([P, n, GROUP])

            def weigh_cells(t):
                return vec.tensor_tensor_reduce(out=weighted[:, t, :], in0=pooled[:, t, :], in1=filt[:, t, :],
                                                scale=1.0, scalar=0.0, op0=ALU.mult, op1=ALU.add,
                                                accum_out=sums[:, t, 0:1])

            def weigh_early(g):
                dve.wait_ge(act_cells, 1 if isinstance(g, int) and g == 0 else 2 * g)
                dve.wait_ge(cells_done, PER * g + 2)
                weigh_cells(0)
                weigh_cells(1)

            def sum_cells(g):
                dve.wait_ge(cells_done, PER * (g + 1))
                weigh_cells(2).then_inc(chain, 1)
                vec.tensor_reduce(sums[:, :, 1], pooled[:, :, :], AX.X, ALU.add).then_inc(chain, 1)
                dve.wait_ge(chain, CHAIN * g + 2)
                each = sums[:, :, :].rearrange("p t (k n) -> p (t k) n", n=1)
                vec.tensor_tensor(by_image[:, :, :, :].rearrange("p t k n -> p (t k) n"),
                                  each.broadcast_to([P, 2 * PER, GROUP]), of_image(2 * PER), ALU.mult).then_inc(sums_done, 1)

            def total_step(g):
                dve.wait_ge(lift_done, g + 1)
                dve.wait_ge(total_mm, g + 1)
                vec.scalar_tensor_tensor(out=total[:, :], in0=lift[:, :], scalar=1.0, in1=p_total,
                                         op0=ALU.add, op1=ALU.mult).then_inc(total_done, 1)

            def gained_step(g):
                dve.wait_ge(taps_mm, g + 1)
                vec.scalar_tensor_tensor(out=taps[:, :, :],
                                         in0=lift[:, :].rearrange("p (k n) -> p k n", k=1).broadcast_to([C, TAPS, GROUP]),
                                         scalar=1.0, in1=p_taps, op0=ALU.add, op1=ALU.mult).then_inc(gained_done, 1)

            def coef_steps(g, slot):
                dve.wait_ge(spread_mm, g + 1)
                vec.tensor_tensor(spread[:, :, :], p_spread, of_image(PER * TAPS), ALU.mult).then_inc(chain, 1)
                dve.wait_ge(chain, CHAIN * g + 3)
                vec.tensor_reduce(coef[:, slot, :, :].rearrange("p t k -> p (t k)"), spread[:, :, :],
                                  AX.X, ALU.add).then_inc(coef_done, 1)

            dve.wait_ge(loaded[0][0], 16)
            sum_direct(0, 0, HEAD_SUMMED)
            dve.wait_ge(gate_tanh, 1)
            vec.tensor_scalar(xg[:, :], gate_act[:, :], 0.0, gate_par[:, 5:6], ALU.max, ALU.add).then_inc(xg_done, 1)
            dve.wait_ge(s_mm, 1)
            vec.reciprocal(inv_s[:, :], p_s).then_inc(assign, 1)
            dve.wait_ge(assign, 1)
            vec.tensor_scalar(share[:, :], xg[:, :], inv_s[:, 0:1], float(C), ALU.mult, ALU.mult).then_inc(assign, 1)
            dve.wait_ge(assign, 2)
            vec.tensor_scalar(count[:, :], share[:, :], ROUND, -ROUND, ALU.add, ALU.add).then_inc(counted, 1)
            dve.wait_ge(narrow_in, 16)
            dve.wait_ge(bounds_mm, 1)
            vec.tensor_tensor(bounds[:, :], p_bounds, edge, ALU.add).then_inc(assign, 1)
            dve.wait_ge(assign, 3)
            vec.tensor_scalar(above[:, :], chan, bounds[:, 0:1], None, ALU.is_ge).then_inc(assign, 1)
            dve.wait_ge(assign, 4)
            vec.scalar_tensor_tensor(out=hit[:, :], in0=chan, scalar=bounds[:, 1:2], in1=above[:, :],
                                     op0=ALU.is_lt, op1=ALU.mult).then_inc(hit_done, 1)
            sum_direct(0, 0, DCT, HEAD_SUMMED).then_inc(cells_done, 1)
            sum_folded(1, 1, half_sums[:, 0], HEAD_FOLDED).then_inc(cells_done, 1)
            dve.wait_ge(later_mm, 1)
            vec.scalar_tensor_tensor(out=chosen[:, :, :].rearrange("p t r -> p (t r)"), in0=p_later, scalar=0.5,
                                     in1=hit[:, :], op0=ALU.is_lt, op1=ALU.mult).then_inc(chosen_done, 1)
            dve.wait_ge(part_in, 16)
            sum_direct(0, 2, HEAD_PART, HEAD_FOLDED)
            sum_folded(2, 2, early_halves, HEAD_FOLDED)
            dve.wait_ge(filt_done, 1)
            weigh_early(0)
            dve.wait_ge(loaded[0][2], 16)
            sum_direct(0, 2, DCT, HEAD_PART).then_inc(cells_done, 1)
            dve.wait_ge(wide_in, 16)
            sum_cells(0)
            total_step(0)
            dve.wait_ge(loaded[1][0], 16)
            sum_direct(1, 0, HEAD_FOLDED)
            gained_step(0)
            sum_folded(3, 0, half_sums[:, 1], DCT, HEAD_FOLDED).then_inc(cells_done, 1)
            coef_steps(0, 0)
            n_pixels = vector_rows(HEAD_ROWS[0]) * W
            dve.wait_ge(coef_done, 1)
            dve.wait_ge(pad_zeroed, 1)
            vec.tensor_scalar(xout[:, 0, 0, 0:n_pixels], xin[:, 0, 0, 0:n_pixels],
                              coef[:, 0, 0, WHOLE_TAP:WHOLE_TAP + 1], bias[:, 0:1], ALU.mult, ALU.add).then_inc(own_tap, 1)

            def tap(turn, s, t, which, first=0, end=None):
                tile = TILES * turn + PER * s + t
                if which == 0:
                    if isinstance(tile, int) and tile == 0:
                        dve.wait_ge(own_tap, 1)
                    else:
                        dve.wait_ge(first_tap, tile)
                elif which == 2 and end is not None:
                    dve.wait_ge(half_tap0_done, t)
                elif which == 3 and end is not None:
                    dve.wait_ge(half_tap2_done, t)
                elif which == 2:
                    dve.wait_ge(tap0_done, tile + 1)
                else:
                    dve.wait_ge(tap2_done, tile + 1)
                upper = end is not None
                if end is None:
                    end = vector_rows(chunk_rows(turn, s)[t])
                irows, cols, ocols = tap_windows(first, end - first, which)
                acc = result(s, t)[:, first:end, ocols]
                ins = vec.scalar_tensor_tensor(out=acc, in0=grid(s, t)[:, irows, cols],
                                               scalar=coef[:, s, t, which:which + 1],
                                               in1=acc, op0=ALU.mult, op1=ALU.add)
                if upper:
                    ins.then_inc({0: half_tap0_done, 2: half_tap2_done, 3: half_rows_done}[which], 1)
                else:
                    ins.then_inc({0: tap0_done, 2: tap2_done, 3: rows_done}[which], 1)

            def turn_of(turn, last):
                for s in range(SLOTS):
                    g = SLOTS * turn + s
                    other = (s + 1) % SLOTS
                    loads = turn + 1 + (s + 1) // SLOTS
                    if last and s == SLOTS - 1:
                        whole, upper, lower = range(3)
                        for t, which, part in [(0, 0, whole), (0, 2, whole), (1, 0, upper), (0, 3, whole),
                                               (1, 2, upper), (1, 0, lower), (1, 3, upper), (1, 2, lower),
                                               (2, 0, upper), (1, 3, lower), (2, 2, upper), (2, 0, lower),
                                               (2, 3, upper), (2, 2, lower), (2, 3, lower)]:
                            tap(turn, s, t, which, *[(0, None), (0, LAST_HALF[t]), (LAST_HALF[t], None)][part])
                        continue
                    if isinstance(turn, int) and g == 0:
                        order = [(0, 0), (0, 2), (0, 3), (1, 0), (1, 2)]
                    else:
                        order = [(0, 0), (1, 0), (0, 2), (1, 2), (0, 3)]
                    for t, which in order:
                        tap(turn, s, t, which)
                    sum_folded(2 * g + 4, 1, half_sums[:, 0], FOLDED[1]).then_inc(cells_done, 1)
                    dve.wait_ge(loaded[other][2], 16 * loads)
                    sum_direct(other, 2, DCT, FOLDED[2])
                    weigh_early(g + 1)
                    sum_folded(2 * g + 5, 2, half_sums[:, 1], FOLDED[2]).then_inc(cells_done, 1)
                    sum_cells(g + 1)
                    tap(turn, s, 1, 3)
                    total_step(g + 1)
                    tap(turn, s, 2, 0)
                    gained_step(g + 1)
                    tap(turn, s, 2, 2)
                    coef_steps(g + 1, other)
                    tap(turn, s, 2, 3)
                    if not last:
                        dve.wait_ge(loaded[s][0], 16 * (turn + 2))
                        sum_direct(s, 0, DCT - SUMMED[0]).then_inc(cells_done, 1)

            turn_of(0, False)
            with dve.Fori(1, TURNS - 1) as turn:
                turn_of(turn, False)
            turn_of(TURNS - 1, True)

        @block.scalar
        def _(act):
            sca = nc.scalar
            def sum_cells(loads, slot, t, rows, copies, end=DCT):
                act.wait_ge(loaded[slot][t], 16 * loads)
                cells = xin[:, slot, t, PAD:].rearrange("p (a b c d) -> p a c b d", a=DCT, b=BLK, c=DCT)
                for cell in range(DCT * (end - rows), DCT * end):
                    ins = sca.activation(copies[:, CELLS - 1 - cell, :, :], cells[:, cell // DCT, cell % DCT, :, :],
                                         ACT.Copy, accum_out=pooled[:, t, cell:cell + 1])
                if end == DCT:
                    ins.then_inc(act_cells, 1)

            act.wait_ge(zeroed, 1)
            sca.activation(gate_act[:, :], zeros[0:NF, 0:1], ACT.Tanh)
            for half in range(2):
                if half == 0:
                    act.wait_ge(folded, 1)
                act.wait_ge(gate_mm, half + 1)
                sca.activation(banks[0:NF, GATE_HALF * half:GATE_HALF * (half + 1), 0:GATE_CHUNK],
                               banks[0:NF, GATE_HALF * half:GATE_HALF * (half + 1), 0:GATE_CHUNK], ACT.Relu,
                               bias=b_gate[:, :], scale=a_gate[:, :],
                               accum_out=gate_sum[:, half:half + 1]).then_inc(gate_relu, 1)
            act.wait_ge(gate2_mm, 1)
            sca.activation(gate_act[:, :], p_gate2, ACT.Tanh, bias=gate_par[:, 4:5],
                           scale=1.0 / HW).then_inc(gate_tanh, 1)
            sum_cells(1, 0, 1, DCT - HEAD_FOLDED, early_pixels)
            act.wait_ge(filt_mm, 1)
            sca.activation(filt[:, :, :].rearrange("p t c -> p (t c)"), p_filt, ACT.Copy).then_inc(filt_done, 1)

            def lift_relu(g):
                act.wait_ge(mixed_mm, g + 1)
                sca.activation(lift[:, :], p_mixed, ACT.Relu, bias=b_chan[:, :],
                               scale=a_chan[:, :]).then_inc(lift_done, 1)

            def hidden_relu(g):
                act.wait_ge(hidden_mm, g + 1)
                sca.activation(hidden[:, :], p_hidden, ACT.Relu, bias=b_hid[:, :],
                               scale=a_hid[:, :]).then_inc(hidden_done, 1)

            def diagonals(turn, s, t):
                act.wait_ge(coef_done, SLOTS * turn + s + 1)
                for w in range(TAPS):
                    ins = sca.activation(diag[:, t, w, :], ident, ACT.Copy, scale=coef[:, s, t, w:w + 1])
                ins.then_inc(diag_done, 1)

            def tap_and_bias(turn, s, t):
                n_rows = vector_rows(chunk_rows(turn, s)[t])
                if not (isinstance(turn, int) and turn == 0):
                    act.wait_ge(stored[s][t], 16 * turn)
                sca.activation(xout[:, s, t, 0:n_rows * W], xin[:, s, t, 0:n_rows * W], ACT.Identity,
                               bias=bias[:, t:t + 1],
                               scale=coef[:, s, t, WHOLE_TAP:WHOLE_TAP + 1]).then_inc(first_tap, 1)

            def start_tile(turn, s, t):
                diagonals(turn, s, t)
                tap_and_bias(turn, s, t)

            def take_psum(turn, s, t):
                act.wait_ge(conv_mm, TILES * turn + PER * s + t + 1)
                rows = chunk_rows(turn, s)
                first = CHUNKS * ((PER * s + t) % 2)
                sca.activation(xout[:, s, t, vector_rows(rows[t]) * W:].rearrange("p (b f) -> p b f", b=CHUNKS),
                               banks[:, first:first + CHUNKS, 0:rows[t] * W], ACT.Identity,
                               bias=bias[:, t:t + 1]).then_inc(conv_out, 1)

            act.wait_ge(folded, 4)
            lift_relu(0)
            hidden_relu(0)
            act.wait_ge(pad_zeroed, 1)
            act.wait_ge(wide_in, 16)
            diagonals(0, 0, 0)

            def turn_of(turn, last):
                for s in range(SLOTS):
                    final = last and s == SLOTS - 1
                    after = (turn + (s + 1) // SLOTS, (s + 1) % SLOTS)
                    if isinstance(turn, int) and SLOTS * turn + s == 0:
                        tap_and_bias(turn, s, 1)
                    diagonals(turn, s, 1)
                    before = 0 if final else HEAD_BEFORE if isinstance(turn, int) and turn == s == 0 else SUMMED[1]
                    if before:
                        sum_cells(after[0] + 1, after[1], 1, before, pixels[:, 1], DCT - SUMMED[1] + before)
                    take_psum(turn, s, 0)
                    if not final and before < SUMMED[1]:
                        sum_cells(after[0] + 1, after[1], 1, SUMMED[1] - before, pixels[:, 1])
                    start_tile(turn, s, 2)
                    if not final:
                        lift_relu(SLOTS * turn + s + 1)
                    take_psum(turn, s, 1)
                    if not final:
                        hidden_relu(SLOTS * turn + s + 1)
                        if not last:
                            sum_cells(turn + 2, s, 0, SUMMED[0], pixels[:, 0])
                        if last:
                            act.wait_ge(coef_done, NGROUP)
                            tap_and_bias(*after, 0)
                            diagonals(*after, 0)
                        else:
                            start_tile(*after, 0)
                    take_psum(turn, s, 2)
                    if not final:
                        tap_and_bias(*after, 1)

            turn_of(0, False)
            with act.Fori(1, TURNS - 1) as turn:
                turn_of(turn, False)
            turn_of(TURNS - 1, True)

        @block.tensor
        def _(pe):
            mm = nc.tensor.matmul
            def warm(products, columns=GATE_CHUNK):
                for _ in range(products):
                    mm(banks[:, 0, 0:columns], zeros[:, 0:P], zeros[:, 0:columns], start=True, stop=True)

            pe.wait_ge(zeroed, 1)
            warm(3)
            pe.wait_ge(early_in, 16)
            for half in range(2):
                for b in range(GATE_HALF * half, GATE_HALF * (half + 1)):
                    if b % 2 == 0:
                        pe.wait_ge(image0_in[b // 2], 16)
                    ins = mm(banks[0:NF, b, 0:GATE_CHUNK], w_gate1,
                             image0[:, GATE_CHUNK * b:GATE_CHUNK * (b + 1)], start=True, stop=True)
                ins.then_inc(gate_mm, 1)
            pe.wait_ge(gate_relu, 2)
            for half in range(2):
                ins = mm(p_gate2, w_gate2, gate_sum[:, half:half + 1], start=(half == 0), stop=(half == 1))
            ins.then_inc(gate2_mm, 1)
            pe.wait_ge(narrow_in, 16)
            pe.wait_ge(xg_done, 1)
            mm(p_s, ones, xg[:, :], start=True, stop=True).then_inc(s_mm, 1)
            pe.wait_ge(counted, 1)
            for b in range(2):
                ins = mm(p_bounds[:, b:b + 1], shift[:, b, :], count[:, :], start=True, stop=True)
            ins.then_inc(bounds_mm, 1)
            pe.wait_ge(hit_done, 1)
            mm(p_later, tri, hit[:, :], start=True, stop=True).then_inc(later_mm, 1)
            pe.wait_ge(chosen_done, 1)
            for t in range(PER):
                ins = mm(p_filt[:, CELLS * t:CELLS * (t + 1)], chosen[:, t, :], basis, start=True, stop=True)
            ins.then_inc(filt_mm, 1)

            def mix(g):
                pe.wait_ge(sums_done, g + 1)
                for t in range(PER):
                    ins = mm(p_mixed, w_mix[:, t, :], by_image[:, t, 0, :], start=(t == 0), stop=(t == PER - 1))
                ins.then_inc(mixed_mm, 1)
                for t in range(PER):
                    ins = mm(p_total, pick[t], by_image[:, t, 1, :], start=(t == 0), stop=(t == PER - 1))
                ins.then_inc(total_mm, 1)

            def hide(g):
                pe.wait_ge(total_done, g + 1)
                mm(p_hidden, w_hid, total[:, :], start=True, stop=True).then_inc(hidden_mm, 1)

            def make_taps(g):
                pe.wait_ge(hidden_done, g + 1)
                for w in range(TAPS):
                    ins = mm(p_taps[:, w, :], w_tap[:, w, :], hidden[:, :], start=True, stop=True)
                ins.then_inc(taps_mm, 1)

            def spread_taps(g):
                pe.wait_ge(gained_done, g + 1)
                for t in range(PER):
                    ins = mm(p_spread[:, TAPS * t:TAPS * (t + 1), :], to_rows[:, t, :], taps[:, :, :],
                             start=True, stop=True)
                ins.then_inc(spread_mm, 1)

            def conv_tap(rows, s, t, chunk, which):
                n = rows[t]
                bank = CHUNKS * ((PER * s + t) % 2) + chunk
                r, cols, ocols = tap_windows(vector_rows(n) + n * chunk, n, which)
                acc = banks[:, bank, 0:n * W].rearrange("p (r c) -> p r c", c=W)
                return mm(acc[:, :, ocols], diag[:, t, which, :], grid(s, t)[:, r, cols],
                          start=(which == WHOLE_TAP), stop=(which == 3))

            TAP_ORDER = [WHOLE_TAP, 0, 2, 3]

            def conv_start(turn, s, t):
                pe.wait_ge(diag_done, TILES * turn + PER * s + t + 1)
                tile = TILES * turn + PER * s + t
                if isinstance(tile, int) and tile < 2:
                    return
                pe.wait_ge(conv_out, tile - 1)

            def conv(turn, s, t, between=()):
                between = dict(between)
                conv_start(turn, s, t)
                for n in range(CHUNKS * TAPS):
                    if n in between:
                        between[n]()
                    ins = conv_tap(chunk_rows(turn, s), s, t, n // TAPS, TAP_ORDER[n % TAPS])
                ins.then_inc(conv_mm, 1)

            warm(2)
            warm(1, 128)
            pe.wait_ge(wide_in, 16)
            mix(0)
            warm(1, 256)
            hide(0)
            warm(1)
            make_taps(0)
            warm(2, 256)
            spread_taps(0)
            warm(2, 256)

            def turn_of(turn, last):
                for s in range(SLOTS):
                    if last and s == SLOTS - 1:
                        for t in range(PER):
                            conv(turn, s, t)
                        continue
                    g = SLOTS * turn + s
                    conv(turn, s, 0)
                    conv(turn, s, 1)
                    conv(turn, s, 2, zip(PATH_AT, [lambda: mix(g + 1), lambda: hide(g + 1),
                                                               lambda: make_taps(g + 1), lambda: spread_taps(g + 1)]))

            turn_of(0, False)
            with pe.Fori(1, TURNS - 1) as turn:
                turn_of(turn, False)
            turn_of(TURNS - 1, True)


def constants():
    import numpy as np
    low_x = [0, 0, 1, 1, 0, 2, 2, 1, 2, 0, 3, 4, 0, 1, 3, 0, 1, 2, 3, 4, 5, 0, 1, 2, 3, 4, 5, 6, 1, 2, 3, 4]
    low_y = [0, 1, 0, 1, 2, 0, 1, 2, 2, 3, 0, 0, 4, 3, 1, 5, 4, 3, 2, 1, 0, 6, 5, 4, 3, 2, 1, 0, 6, 5, 4, 3]

    def wave(freq):
        f = np.array(freq, np.float64)[:, None]
        r = np.cos(np.pi * f * (np.arange(DCT)[None, :] + 0.5) / DCT) / np.sqrt(DCT)
        return np.where(f == 0, r, r * np.sqrt(2.0))

    k = np.zeros((NF, N_END), np.float32)
    k[:, N_ONES:N_SHIFT] = 1.0
    low, high = np.zeros((NF, NF)), np.zeros((NF, NF))
    for i in range(NF - 1):
        low[i, i + 1] = 1.0
        high[i, i] = 1.0
        high[i, NF - 1] = -1.0
    k[:, N_SHIFT:N_SHIFT + NF] = low
    k[:, N_SHIFT + NF:N_TRI] = high
    k[NF - 1, N_EDGE + 1] = C
    k[:, N_TRI:N_EDGE] = np.tril(np.ones((NF, NF)), -1)
    rows = np.arange(P)
    for t in range(PER):
        k[:, N_CHAN + P * t:N_CHAN + P * (t + 1)] = PER * (rows % QUAD) + t
    basis = wave(low_x)[:, :, None] * wave(low_y)[:, None, :]
    k[:, N_BASIS:N_TAP] = basis.reshape(NF, CELLS) / (BLK * BLK)

    w = np.zeros((P, W_END), np.float32)
    w[:, W_IDENT:W_IMAGE] = np.eye(P)
    w[:, W_IMAGE:W_PICK] = rows[:, None] // QUAD == np.arange(GROUP)
    w[:, W_PICK + (PER - 1) * QUAD:][:, :QUAD] = rows[:, None] % QUAD == np.arange(QUAD)
    for t in range(PER):
        w[QUAD * t:QUAD * (t + 1), W_SPREAD + P * t:W_SPREAD + P * (t + 1)] = np.arange(QUAD)[:, None] == rows % QUAD
    return k, w


def kernel(x, L0_conv_wg1, L0_conv_bn2_g, L0_conv_bn2_b, L0_conv_bn2_m, L0_conv_bn2_v, L0_conv_wg2,
           L0_conv_bg2, L0_conv_beta, L0_conv_w1d, L0_conv_b1d, L0_conv_bn1_g, L0_conv_bn1_b, L0_conv_bn1_m,
           L0_conv_bn1_v, L1_conv_w1, L1_conv_gamma, L1_conv_beta, L1_conv_running_mean,
           L1_conv_running_var, L1_conv_w2, L1_conv_b2, L1_conv_bias):
    import numpy as np
    import concourse.bacc as bacc
    from concourse.bass_utils import run_bass_kernel_spmd as run

    a = np.asarray
    by_tile = lambda v: v.reshape((QUAD, PER) + v.shape[1:]).swapaxes(0, 1).reshape(v.shape)
    narrow, wide = constants()
    early = np.zeros((C, E_END), np.float32)
    early[:, E_GATE1:E_GATE2] = a(L0_conv_wg1).T
    early[:NF, E_GATE2:E_CHAN] = a(L0_conv_wg2).T
    early[:, E_CHAN:E_GATE] = by_tile(np.stack([a(L0_conv_b1d), a(L0_conv_bn1_m), a(L0_conv_bn1_g),
                                                a(L0_conv_bn1_b), a(L0_conv_bn1_v)], axis=1))
    early[:NF, E_GATE:E_HID] = np.stack([a(L0_conv_bn2_g), a(L0_conv_bn2_b), a(L0_conv_bn2_m), a(L0_conv_bn2_v),
                                         a(L0_conv_bg2), np.repeat(a(L0_conv_beta), NF)], axis=1)
    early[:RED, E_HID:E_END] = np.stack([a(L1_conv_gamma), a(L1_conv_beta), a(L1_conv_running_mean),
                                         a(L1_conv_running_var)], axis=1)
    early[RED:HID, E_END - 1] = 1.0
    early[RED, E_HID + 1] = 1.0
    make = np.zeros((HID, TAPS, C), np.float32)
    make[:RED] = by_tile(a(L1_conv_w2).reshape(C, 9, RED)).transpose(2, 1, 0)[:, :TAPS]
    make[RED] = by_tile(a(L1_conv_b2).reshape(C, 9)).T[:TAPS]
    narrow[:, N_TAP:N_END] = make.reshape(HID, TAPS * C)
    mix = by_tile(a(L0_conv_w1d)[:, :, 1]).T.reshape(QUAD, PER * C)
    wide[:, W_BIAS:W_MIX] = np.tile(a(L1_conv_bias).reshape(QUAD, PER), (GROUP, 1))
    wide[:, W_MIX:W_HIDE] = np.tile(mix, (GROUP, 1))
    wide[:C, W_HIDE:W_HIDE + RED] = by_tile(a(L1_conv_w1).T)
    arrays = {"x": a(x), "early": early, "narrow": narrow, "wide": wide}
    arrays = {name: np.ascontiguousarray(v) for name, v in arrays.items()}
    nc = bacc.Bacc("TRN2", target_bir_lowering=False, num_devices=1)
    args = [nc.dram_tensor(name, v.shape, mybir.dt.float32, kind="ExternalInput").ap() for name, v in arrays.items()]
    out = nc.dram_tensor("out", (NIMG, C, H, W), mybir.dt.float32, kind="ExternalOutput").ap()
    build(nc, *args, out)
    r = run(nc, [arrays], core_ids=[0])
    return r.results[0]["out"]
```
